# Optimizing a Trainium2 kernel written in Bass

```python
import numpy as np
import jax
import jax.numpy as jnp

def _softmax(x, axis=-1):
    return jax.nn.softmax(x, axis=axis)

def _gelu(x):
    return jax.nn.gelu(x, approximate=True)

def _silu(x):
    return jax.nn.silu(x)

def _sigmoid(x):
    return jax.nn.sigmoid(x)

def _layernorm(x, axis=-1, eps=1e-05):
    m = jnp.mean(x, axis=axis, keepdims=True)
    v = jnp.var(x, axis=axis, keepdims=True)
    return (x - m) / jnp.sqrt(v + eps)

def _scatter_add(tgt, idx, src, axis=0):
    return tgt.at[idx].add(src)

def _segment_sum(src, seg, n):
    return jax.ops.segment_sum(src, seg, n)
kernel_name = 'mk_audio_tower_d1_tok_aud1d512_r4_9e9fda'

def setup_inputs(seed: int=0):
    np.random.seed(seed)
    _w = jnp.asarray

    def _rec_inputs():
        import jax
        import jax.numpy as jnp
        _rk = jax.random.key(seed)
        x = -0.00238186 + 1.00146 * jax.random.normal(jax.random.fold_in(_rk, 1), (64, 5000), jnp.float32)
        return x
    x = _rec_inputs()

    def _L0_tok_setup():
        import jax, jax.numpy as jnp
        import numpy as np
        B, E, G, P = (8, 16, 5000, 128)
        MASK_DENSITY = 0.1
        key = jax.random.key(seed)
        k_x, k_w, k_m = jax.random.split(key, 3)
        x = jax.random.normal(k_x, (B, G), dtype=jnp.float32)
        weight = jax.random.normal(k_w, (E, G, P), dtype=jnp.float32) * 0.01
        bias = jnp.zeros((E, P), dtype=jnp.float32)
        mask = (jax.random.uniform(k_m, (G, P)) < MASK_DENSITY).astype(jnp.float32)
        return {'x': x, 'weight': weight, 'bias': bias, 'mask': mask}
    _L0_tok_all = _L0_tok_setup()
    _L0_tok_in = {k: v for k, v in _L0_tok_all.items() if k in ('weight', 'bias', 'mask')}
    del _L0_tok_all

    def _L0_attn_setup():
        import jax, jax.numpy as jnp
        import numpy as np
        EPS = 1e-12
        key = jax.random.key(seed)
        x = jax.random.normal(key, (8, 512, 128), dtype=jnp.float32)
        return {'x': x}
    _L0_attn_all = _L0_attn_setup()
    _L0_attn_in = {k: v for k, v in _L0_attn_all.items() if k in ()}
    del _L0_attn_all

    def _L0_ffn_setup():
        import jax, jax.numpy as jnp
        import numpy as np
        B, S, D, F, E, NS, K = (2, 512, 128, 512, 8, 2, 2)
        key = jax.random.key(seed)
        ks = jax.random.split(key, 6)
        scale = 0.02

        def p(k, shape):
            return jax.random.normal(k, shape, jnp.float32) * scale
        return {'x': jax.random.normal(ks[0], (B, S, D), jnp.float32), 'gate_w': p(ks[1], (E, D)), 'gate_b': jnp.zeros((E,), jnp.float32), 'sw1': p(ks[2], (NS, F, D)), 'sb1': jnp.zeros((NS, F), jnp.float32), 'sw2': p(ks[3], (NS, D, F)), 'sb2': jnp.zeros((NS, D), jnp.float32), 'rw1': p(ks[4], (E, F, D)), 'rb1': jnp.zeros((E, F), jnp.float32), 'rw2': p(ks[5], (E, D, F)), 'rb2': jnp.zeros((E, D), jnp.float32)}
    _L0_ffn_all = _L0_ffn_setup()
    _L0_ffn_in = {k: v for k, v in _L0_ffn_all.items() if k in ('gate_w', 'gate_b', 'sw1', 'sb1', 'sw2', 'sb2', 'rw1', 'rb1', 'rw2', 'rb2')}
    del _L0_ffn_all
    return {'x': x, 'L0_tok_weight': _L0_tok_in['weight'], 'L0_tok_bias': _L0_tok_in['bias'], 'L0_tok_mask': _L0_tok_in['mask'], 'L0_ffn_gate_w': _L0_ffn_in['gate_w'], 'L0_ffn_gate_b': _L0_ffn_in['gate_b'], 'L0_ffn_sw1': _L0_ffn_in['sw1'], 'L0_ffn_sb1': _L0_ffn_in['sb1'], 'L0_ffn_sw2': _L0_ffn_in['sw2'], 'L0_ffn_sb2': _L0_ffn_in['sb2'], 'L0_ffn_rw1': _L0_ffn_in['rw1'], 'L0_ffn_rb1': _L0_ffn_in['rb1'], 'L0_ffn_rw2': _L0_ffn_in['rw2'], 'L0_ffn_rb2': _L0_ffn_in['rb2']}

def reference(x, L0_tok_weight, L0_tok_bias, L0_tok_mask, L0_ffn_gate_w, L0_ffn_gate_b, L0_ffn_sw1, L0_ffn_sb1, L0_ffn_sw2, L0_ffn_sb2, L0_ffn_rw1, L0_ffn_rb1, L0_ffn_rw2, L0_ffn_rb2):
    import jax
    import jax.numpy as jnp

    def _L0_tok_ref(x, weight, bias, mask):
        import jax, jax.numpy as jnp
        import numpy as np
        B, E, G, P = (8, 16, 5000, 128)
        MASK_DENSITY = 0.1
        W = weight * mask[None, :, :]
        out = jnp.einsum('bg,egp->bep', x, W)
        return out + bias[None, :, :]

    def _L0_attn_ref(x):
        import jax, jax.numpy as jnp
        import numpy as np
        EPS = 1e-12
        xn = x / (jnp.linalg.norm(x, axis=-1, keepdims=True) + EPS)
        scores = jnp.einsum('bid,bjd->bij', xn, xn)
        scores = scores * scores
        weights = jax.nn.softmax(scores, axis=-1)
        context = jnp.einsum('bij,bjd->bid', weights, x)
        return context

    def _L0_ffn_ref(x, gate_w, gate_b, sw1, sb1, sw2, sb2, rw1, rb1, rw2, rb2):
        import jax, jax.numpy as jnp
        import numpy as np
        B, S, D, F, E, NS, K = (2, 512, 128, 512, 8, 2, 2)
        b, s, d = x.shape
        t = x.reshape(-1, d)
        T = t.shape[0]
        hs = jax.nn.gelu(jnp.einsum('td,nfd->ntf', t, sw1) + sb1[:, None, :], approximate=False)
        shared = jnp.einsum('ntf,ndf->td', hs, sw2) + sb2.sum(axis=0)
        logits = t @ gate_w.T + gate_b
        probs = jax.nn.softmax(logits, axis=-1)
        top_v, top_i = jax.lax.top_k(probs, K)
        cw = jnp.zeros_like(probs).at[jnp.arange(T)[:, None], top_i].add(top_v)
        hr = jax.nn.gelu(jnp.einsum('td,efd->etf', t, rw1) + rb1[:, None, :], approximate=False)
        oe = jnp.einsum('etf,edf->etd', hr, rw2) + rb2[:, None, :]
        routed = jnp.einsum('etd,te->td', oe, cw)
        return (shared + routed).reshape(b, s, d)
    h = _L0_tok_ref(x, L0_tok_weight, L0_tok_bias, L0_tok_mask)
    h = h + _L0_attn_ref(_layernorm(h, axis=-1))
    h = h + _L0_ffn_ref(_layernorm(h, axis=-1), L0_ffn_gate_w, L0_ffn_gate_b, L0_ffn_sw1, L0_ffn_sb1, L0_ffn_sw2, L0_ffn_sb2, L0_ffn_rw1, L0_ffn_rb1, L0_ffn_rw2, L0_ffn_rb2)
    return h

_drawn_inputs = setup_inputs


def setup_inputs(seed=0):
    import zlib

    import numpy as np

    out = dict(_drawn_inputs(seed))
    spreads = {'L0_tok_bias': (0.0, 0.1),
     'L0_ffn_gate_b': (0.0, 0.1),
     'L0_ffn_sb1': (0.0, 0.1),
     'L0_ffn_sb2': (0.0, 0.1),
     'L0_ffn_rb1': (0.0, 0.668),
     'L0_ffn_rb2': (0.0, 0.1)}
    factors = {}
    for name, (base, spread) in spreads.items():
        noise = np.random.default_rng([zlib.crc32(name.encode()), seed]).standard_normal(out[name].shape)
        drawn = base * np.exp(spread * noise) if base else spread * noise
        out[name] = jnp.asarray(drawn.astype(out[name].dtype))
    for name, factor in factors.items():
        out[name] = (out[name] * factor).astype(out[name].dtype)
    return out
```

```python
import concourse.bass as bass
from concourse import mybir
from contextlib import ExitStack

F32 = mybir.dt.float32
F32R = mybir.dt.float32r
ALU = mybir.AluOpType
ACT = mybir.ActivationFunctionType
AX = mybir.AxisListType

P = 128
B, E, G = 64, 16, 5000
CHUNKS = G // P
REST = G - CHUNKS * P
WCOLS = E * P
TCOLS = WCOLS + P + B
RING = 6
LOOPS = CHUNKS // RING
TAIL = CHUNKS - LOOPS * RING
TOK = B * E
TILES = TOK // P
HALF = TOK // 2
NS, NR = 2, 8
NX = NS + NR
FF = 512
FB = FF // P
WX = FF + FB * P
XB = FB + 1
LN_EPS = 1e-05
NORM_EPS = 1e-12


def build(nc, tiles, rest, tok_bias, experts, gate_w, gate_b, out):
    ctx = ExitStack()
    with ctx:
        def sb(name, shape, dt=F32):
            return ctx.enter_context(nc.sbuf_tensor(name, shape, dt))

        def sem(name):
            return ctx.enter_context(nc.semaphore(name))

        ring = sb("ring", [P, RING, TCOLS])
        rest_tile = sb("rest_tile", [REST, TCOLS])
        bias_rows = sb("bias_rows", [P, TILES, P])
        ident = sb("ident", [P, P])
        block_mask = sb("block_mask", [P, P])
        lower = sb("lower", [P, NR, NR])
        ones = sb("ones", [P, P])
        half_power = sb("half_power", [P, 2, TILES])
        gate_w_sb = sb("gate_w_sb", [P, NR])
        gate_b_sb = sb("gate_b_sb", [1, NR])
        zeros = sb("zeros", [P, XB])
        h_rows = sb("h_rows", [P, TILES, P])
        h_cols = sb("h_cols", [P, B, E])
        h_tok = sb("h_tok", [P, TILES, P])
        hn = sb("hn", [P, TILES, P])
        xn = sb("xn", [P, TILES, P])
        xn_cols = sb("xn_cols", [P, TILES, P])
        sq = sb("sq", [P, TILES, P])
        ex = sb("ex", [P, TILES, P])
        attn = sb("attn", [P, TILES, P])
        h2 = sb("h2", [P, TILES, P])
        t_tok = h_rows
        t_cols = sb("t_cols", [P, TOK])
        t_hi = sb("t_hi", [P, TOK], F32R)
        t_lo = sb("t_lo", [P, TOK], F32R)
        stats = sb("stats", [P, 2, TILES, 6])
        mv = sb("mv", [P, 2, TILES, 2])
        base = sb("base", [P, 3, TILES])
        root = sb("root", [P, 3, TILES])
        small = sb("small", [P, 4, TILES])
        g_max = sb("g_max", [P, TILES])
        g_sh = sb("g_sh", [P, TILES, NR])
        g_ex = sb("g_ex", [P, TILES, NR])
        g_sum = sb("g_sum", [P, 2, TILES])
        cmp_ge = sb("cmp_ge", [P, TILES, NR * NR])
        cmp_gt = sb("cmp_gt", [P, TILES, NR * NR])
        rank = sb("rank", [P, 3, TILES, NR])
        cw = sb("cw", [P, TILES, NR])
        cw_cols = sb("cw_cols", [NR, TOK])
        one_rows = sb("one_rows", [NS, TOK])
        cw_dram = nc.dram_tensor("cw_dram", [NX, TOK], F32, kind="Internal").ap()
        w_raw = sb("w_raw", [P, 2, WX + XB])
        bias_now = sb("bias_now", [P, 2, XB])
        w_hi = sb("w_hi", [P, 2, WX], F32R)
        w_lo = sb("w_lo", [P, 2, WX], F32R)
        over = ring[:, :, :].rearrange("p r c -> p (r c)")
        act = over[:, 0:2 * FB * HALF].rearrange("p (s c) -> p s c", s=2)
        act_hi = sb("act_hi", [P, 2, FB * HALF], F32R)
        act_lo = sb("act_lo", [P, 2, FB * HALF], F32R)
        cwb = over[:, 2 * FB * HALF:2 * FB * HALF + 2 * TOK].rearrange("p (s c) -> p s c", s=2)
        part = sb("part", [P, 2, HALF])
        acc = sb("acc", [P, TOK])
        y = sb("y", [P, TILES, P])

        banks = [ctx.enter_context(nc.psum_tensor(f"bank{n}", [P, 512], F32)) for n in range(8)]

        tile_loaded = [sem(f"tile_loaded{r}") for r in range(RING)]
        rest_loaded = sem("rest_loaded")
        rest_masked = sem("rest_masked")
        masked = sem("masked")
        chunk_used = sem("chunk_used")
        h_summed = sem("h_summed")
        bias_loaded = sem("bias_loaded")
        gate_loaded = sem("gate_loaded")
        const_step = sem("const_step")
        h_added = sem("h_added")
        hT_done = sem("hT_done")
        hT_copied = [sem("hT_copied0"), sem("hT_copied1")]
        htok_done = sem("htok_done")
        htok_copied = sem("htok_copied")
        dve_link = sem("dve_link")
        base_ready = sem("base_ready")
        root_ready = sem("root_ready")
        scales_ready = sem("scales_ready")
        hn_ready = sem("hn_ready")
        xn_ready = sem("xn_ready")
        xnT_done = sem("xnT_done")
        xnT_copied = sem("xnT_copied")
        gram_done = sem("gram_done")
        sq_done = sem("sq_done")
        ex_done = sem("ex_done")
        attn_ready = sem("attn_ready")
        ctx_done = sem("ctx_done")
        h2_ready = sem("h2_ready")
        t_ready = sem("t_ready")
        tT_done = sem("tT_done")
        t_copied = sem("t_copied")
        t_split = sem("t_split")
        logits_done = sem("logits_done")
        g_shifted = sem("g_shifted")
        g_exped = sem("g_exped")
        cw_ready = sem("cw_ready")
        cwT_done = sem("cwT_done")
        cw_copied = sem("cw_copied")
        cw_stored = sem("cw_stored")
        w_loaded = [sem("w_loaded0"), sem("w_loaded1")]
        w_rounded = sem("w_rounded")
        w_split = sem("w_split")
        cwb_loaded = [sem("cwb_loaded0"), sem("cwb_loaded1")]
        up_done = sem("up_done")
        gelu_done = sem("gelu_done")
        act_rounded = sem("act_rounded")
        act_split = sem("act_split")
        down_done = sem("down_done")
        part_ready = sem("part_ready")
        acc_done = sem("acc_done")
        yT_done = sem("yT_done")
        y_ready = sem("y_ready")
        out_stored = sem("out_stored")

        block = ctx.enter_context(nc.Block())

        def after(eng, s, value):
            if not isinstance(value, int) or value > 0:
                eng.wait_ge(s, value)

        def turns(eng, body):
            body(0)
            with eng.Fori(1, NX // 2 - 1) as i:
                body(i)
            body(NX // 2 - 1)

        @block.sync
        def _(eng):
            eng.dma_start(rest_tile[:, :], rest).then_inc(rest_loaded, 16)
            for r in range(RING):
                eng.dma_start(ring[:, r, :], tiles[r]).then_inc(tile_loaded[r], 16)
            with eng.Fori(1, LOOPS) as i:
                for r in range(RING):
                    eng.wait_ge(chunk_used, RING * i + (r + 1 - RING))
                    eng.dma_start(ring[:, r, :], tiles[bass.ds(RING * i + r, 1)].rearrange("a p c -> (a p) c"))\
                       .then_inc(tile_loaded[r], 16)
            for r in range(TAIL):
                eng.wait_ge(chunk_used, RING * (LOOPS - 1) + r + 1)
                eng.dma_start(ring[:, r, :], tiles[RING * LOOPS + r]).then_inc(tile_loaded[r], 16)
            for x in range(2):
                eng.dma_start(w_raw[:, x, :], experts[x]).then_inc(w_loaded[x], 16)
            eng.wait_ge(const_step, 1)
            eng.dma_start(cw_dram[0:NS, :], one_rows[:, :]).then_inc(cw_stored, 16)
            eng.wait_ge(cw_copied, 2)
            eng.dma_start(cw_dram[NS:NX, :], cw_cols[:, :]).then_inc(cw_stored, 16)
            eng.wait_ge(cw_stored, 32)

            def turn(i):
                for s in range(2):
                    x = 2 * i + s
                    after(eng, part_ready, 2 * x - 2)
                    eng.dma_start(cwb[:, s, :], cw_dram[bass.ds(x, 1), :].to_broadcast([P, TOK]))\
                       .then_inc(cwb_loaded[s], 16)
                    if not isinstance(i, int) or i < NX // 2 - 1:
                        eng.wait_ge(w_split, x + 1)
                        eng.dma_start(w_raw[:, s, :], experts[bass.ds(x + 2, 1)].rearrange("a p c -> (a p) c"))\
                           .then_inc(w_loaded[s], 16)
            turns(eng, turn)
            for q in range(2):
                eng.wait_ge(y_ready, q + 1)
                eng.dma_start(out.rearrange("(t p) d -> p t d", p=P)[:, 4 * q:4 * q + 4, :],
                              y[:, 4 * q:4 * q + 4, :]).then_inc(out_stored, 16)
            eng.wait_ge(out_stored, 32)

        @block.gpsimd
        def _(eng):
            eng.memset(one_rows[:, :], 1.0).then_inc(const_step, 1)
            eng.memset(ident[:, :], 0.0)
            eng.memset(block_mask[:, :], 1.0)
            eng.memset(lower[:, :, :], 1.0)
            eng.memset(ones[:, :], 1.0)
            eng.memset(zeros[:, :], 0.0)
            eng.memset(half_power[:, 0, :], -0.5)
            eng.memset(half_power[:, 1, :], 0.5)
            eng.memset(acc[:, :], 0.0).then_inc(const_step, 1)
            eng.wait_ge(const_step, 2)
            eng.affine_select(out=ident[:, :], in_=ident[:, :], compare_op=ALU.not_equal, fill=1.0,
                              base=0, pattern=[[-1, P]], channel_multiplier=1)
            bm = block_mask[:, :].rearrange("p (n e) -> p n e", e=E)
            eng.affine_select(out=bm, in_=bm, compare_op=ALU.is_ge, fill=0.0, base=0,
                              pattern=[[-E, P // E], [0, E]], channel_multiplier=1).then_inc(const_step, 1)
            eng.affine_select(out=lower[:, :, :], in_=lower[:, :, :], compare_op=ALU.is_gt, fill=0.0, base=0,
                              pattern=[[1, NR], [-1, NR]], channel_multiplier=0)
            eng.wait_ge(const_step, 3)
            eng.affine_select(out=bm, in_=bm, compare_op=ALU.is_ge, fill=0.0, base=E - 1,
                              pattern=[[E, P // E], [0, E]], channel_multiplier=-1).then_inc(const_step, 1)

            def split_weights(s, x):
                eng.wait_ge(w_loaded[s], 8 * (x - s) + 16 if isinstance(x, int) else 8 * x + (16 - 8 * s))
                after(eng, down_done, 2 * x - 2)
                eng.tensor_tensor(bias_now[:, s, :], w_raw[:, s, WX:], zeros[:, :], ALU.add)
                eng.tensor_copy(w_hi[:, s, :], w_raw[:, s, 0:WX]).then_inc(w_rounded, 1)
                eng.wait_ge(w_rounded, x + 1)
                eng.tensor_tensor(w_lo[:, s, :], w_raw[:, s, 0:WX], w_hi[:, s, :].bitcast(F32), ALU.subtract)\
                   .then_inc(w_split, 1)

            for x in range(2):
                split_weights(x, x)
            eng.wait_ge(base_ready, 1)
            eng.tensor_tensor(root[:, 0, :], base[:, 0, :], half_power[:, 0, :], ALU.pow)
            eng.tensor_tensor(root[:, 1, :], base[:, 1, :], half_power[:, 1, :], ALU.pow).then_inc(root_ready, 1)
            eng.wait_ge(root_ready, 1)
            eng.wait_ge(htok_copied, 2)
            for t in range(TILES):
                eng.tensor_scalar(hn[:, t, :], h_tok[:, t, :], mv[:, 0, t, 0:1], root[:, 0, t:t + 1],
                                  ALU.subtract, ALU.mult).then_inc(hn_ready, 1)
            eng.wait_ge(base_ready, 2)
            eng.tensor_tensor(root[:, 2, :], base[:, 2, :], half_power[:, 0, :], ALU.pow).then_inc(root_ready, 1)

            def turn(i):
                for j in range(4):
                    k = 4 * i + j
                    eng.wait_ge(part_ready, k + 1)
                    after(eng, acc_done, k - 1)
                    half = acc[:, (j % 2) * HALF:(j % 2 + 1) * HALF]
                    eng.tensor_tensor(half, half, part[:, j % 2, :], ALU.add).then_inc(acc_done, 1)
                    if j % 2 and (not isinstance(i, int) or i < NX // 2 - 1):
                        split_weights(j // 2, 2 * i + (j // 2 + 2))
            turns(eng, turn)

        @block.scalar
        def _(eng):
            for el in range(2):
                eng.dma_start(bias_rows[el * B:(el + 1) * B, :, :],
                              tok_bias[el:el + 1].to_broadcast([B, TILES * P]).rearrange("p (t d) -> p t d", d=P))\
                   .then_inc(bias_loaded, 16)
            eng.dma_start(gate_w_sb[:, :], gate_w).then_inc(gate_loaded, 16)
            eng.dma_start(gate_b_sb[:, :], gate_b).then_inc(gate_loaded, 16)
            eng.wait_ge(hT_done, 1)
            for el in range(2):
                a = eng.activation(h_cols[:, :, el * 8:el * 8 + 4],
                                   banks[2][:, :].rearrange("p (h l b) -> p l b h", h=4, l=2)[:, el],
                                   ACT.Copy)
                a.then_inc(hT_copied[0], 1)
            for q in range(2):
                eng.wait_ge(htok_done, q + 1)
                eng.activation(h_tok[:, 4 * q:4 * q + 4, :], banks[4 + q][:, :].rearrange("p (t d) -> p t d", d=P),
                               ACT.Copy).then_inc(htok_copied, 1)
            for q in range(2):
                eng.wait_ge(xnT_done, q + 1)
                eng.activation(xn_cols[:, 4 * q:4 * q + 4, :], banks[6 + q][:, :].rearrange("p (t d) -> p t d", d=P),
                               ACT.Copy).then_inc(xnT_copied, 1)
            for q in range(2):
                eng.wait_ge(gram_done, q + 1)
                eng.activation(sq[:, 4 * q:4 * q + 4, :], banks[q][:, :].rearrange("p (t d) -> p t d", d=P),
                               ACT.Square).then_inc(sq_done, 1)
                eng.wait_ge(sq_done, q + 1)
                eng.activation(ex[:, 4 * q:4 * q + 4, :], sq[:, 4 * q:4 * q + 4, :], ACT.Exp).then_inc(ex_done, 1)
            for q in range(2):
                eng.wait_ge(tT_done, q + 1)
                eng.activation(t_cols[:, q * HALF:(q + 1) * HALF], banks[6 + q][:, :], ACT.Copy).then_inc(t_copied, 1)
            eng.wait_ge(g_shifted, 1)
            eng.activation(g_ex[:, :, :], g_sh[:, :, :], ACT.Exp).then_inc(g_exped, 1)
            def gelu(i, j):
                k = 4 * i + j
                after(eng, act_split, 2 * k - 2)
                for fb in range(FB):
                    eng.wait_ge(up_done, FB * k + (fb + 1))
                    eng.activation(act[:, j % 2, fb * HALF:(fb + 1) * HALF], banks[fb][:, :], ACT.Gelu,
                                   bias=bias_now[:, j // 2, fb:fb + 1])\
                       .then_inc(gelu_done, 1)

            def turn(i):
                for j in range(4):
                    gelu(i, j)
                    if isinstance(i, int) and i == 0 and j == 0:
                        for q in range(2):
                            eng.wait_ge(cwT_done, q + 1)
                            eng.activation(cw_cols[:, q * HALF:(q + 1) * HALF], banks[6 + q][0:NR, :], ACT.Copy)\
                               .then_inc(cw_copied, 1)
            turns(eng, turn)

        @block.vector
        def _(eng):
            links = [0]

            def link(ins):
                links[0] += 1
                ins.then_inc(dve_link, 1)
                eng.wait_ge(dve_link, links[0])

            def apply_mask(tile, parts, e0, e1):
                w = tile[:, e0 * P:e1 * P].rearrange("p (e d) -> p e d", d=P)
                m = tile[:, WCOLS:WCOLS + P].rearrange("p (o d) -> p o d", o=1).to_broadcast([parts, e1 - e0, P])
                return eng.tensor_tensor(w, w, m, ALU.mult)

            eng.wait_ge(rest_loaded, 16)
            apply_mask(rest_tile, REST, 0, E).then_inc(rest_masked, 1)
            with eng.Fori(0, LOOPS) as i:
                for r in range(RING):
                    eng.wait_ge(tile_loaded[r], 16 * i + 16)
                    apply_mask(ring[:, r, :], P, 0, E).then_inc(masked, 1)
            for r in range(TAIL):
                eng.wait_ge(tile_loaded[r], 16 * LOOPS + 16)
                if r < TAIL - 1:
                    apply_mask(ring[:, r, :], P, 0, E).then_inc(masked, 1)
                else:
                    for q in range(2):
                        apply_mask(ring[:, r, :], P, 8 * q, 8 * q + 8).then_inc(masked, 1)

            eng.wait_ge(bias_loaded, 32)
            for q in range(2):
                eng.wait_ge(h_summed, q + 1)
                eng.tensor_tensor(h_rows[:, 4 * q:4 * q + 4, :], banks[q][:, :].rearrange("p (t d) -> p t d", d=P),
                                  bias_rows[:, 4 * q:4 * q + 4, :], ALU.add).then_inc(h_added, 1)
            eng.wait_ge(hT_done, 2)
            for el in range(2):
                eng.tensor_copy(h_cols[:, :, el * 8 + 4:el * 8 + 8],
                                banks[3][:, :].rearrange("p (h l b) -> p l b h", h=4, l=2)[:, el])\
                   .then_inc(hT_copied[1], 1)

            def norm_stats(n, src, ready):
                for t in range(TILES):
                    if t % 4 == 0:
                        eng.wait_ge(ready, t // 4 + 1)
                    s = eng.bn_stats(stats[:, n, t, :], src(t))
                link(s)
                for t in range(TILES):
                    s = eng.bn_aggr(mv[:, n, t, :], stats[:, n, t, :])
                link(s)

            norm_stats(0, lambda t: h_tok[:, t, :], htok_copied)
            eng.tensor_scalar(base[:, 0, :], mv[:, 0, :, 1], LN_EPS, None, ALU.add)
            eng.tensor_scalar(base[:, 1, :], mv[:, 0, :, 1], float(P), None, ALU.mult).then_inc(base_ready, 1)
            eng.wait_ge(root_ready, 1)
            link(eng.tensor_tensor(small[:, 0, :], root[:, 0, :], root[:, 1, :], ALU.mult))
            link(eng.tensor_scalar(small[:, 1, :], small[:, 0, :], NORM_EPS, None, ALU.add))
            link(eng.reciprocal(small[:, 2, :], small[:, 1, :]))
            link(eng.tensor_tensor(small[:, 3, :], small[:, 2, :], root[:, 0, :], ALU.mult))
            for t in range(TILES):
                eng.tensor_scalar(xn[:, t, :], h_tok[:, t, :], mv[:, 0, t, 0:1], small[:, 3, t:t + 1],
                                  ALU.subtract, ALU.mult).then_inc(xn_ready, 1)
            eng.wait_ge(const_step, 4)
            for q in range(2):
                eng.wait_ge(ex_done, q + 1)
                m = block_mask[:, :].rearrange("p (o d) -> p o d", o=1).to_broadcast([P, 4, P])
                eng.tensor_tensor(attn[:, 4 * q:4 * q + 4, :], ex[:, 4 * q:4 * q + 4, :], m, ALU.mult)\
                   .then_inc(attn_ready, 1)
            for q in range(2):
                eng.wait_ge(ctx_done, q + 1)
                link(eng.reciprocal(g_sum[:, 0, 4 * q:4 * q + 4], banks[4 + q][:, 0:4]))
                for t in range(4 * q, 4 * q + 4):
                    s = eng.scalar_tensor_tensor(out=h2[:, t, :], in0=banks[2 + q][:, (t % 4) * P:(t % 4 + 1) * P],
                                                 scalar=g_sum[:, 0, t:t + 1], in1=h_tok[:, t, :],
                                                 op0=ALU.mult, op1=ALU.add)
                s.then_inc(h2_ready, 1)
            norm_stats(1, lambda t: h2[:, t, :], h2_ready)
            eng.tensor_scalar(base[:, 2, :], mv[:, 1, :, 1], LN_EPS, None, ALU.add).then_inc(base_ready, 1)
            eng.wait_ge(root_ready, 2)
            for t in range(TILES):
                eng.tensor_scalar(t_tok[:, t, :], h2[:, t, :], mv[:, 1, t, 0:1], root[:, 2, t:t + 1],
                                  ALU.subtract, ALU.mult).then_inc(t_ready, 1)
            for q in range(2):
                cols = slice(q * HALF, (q + 1) * HALF)
                eng.wait_ge(t_copied, q + 1)
                link(eng.tensor_copy(t_hi[:, cols], t_cols[:, cols]))
                eng.tensor_tensor(t_lo[:, cols], t_cols[:, cols], t_hi[:, cols].bitcast(F32), ALU.subtract)\
                   .then_inc(t_split, 1)

            eng.wait_ge(logits_done, 1)
            logits = banks[5][:, 0:TILES * NR].rearrange("p (t e) -> p t e", e=NR)
            link(eng.tensor_reduce(g_max[:, :], logits, AX.X, ALU.max))
            per_tile = lambda a: a.rearrange("p (t o) -> p t o", o=1).to_broadcast([P, TILES, NR])
            eng.tensor_tensor(g_sh[:, :, :], logits, per_tile(g_max[:, :]), ALU.subtract).then_inc(g_shifted, 1)

            def router():
                eng.wait_ge(g_exped, 1)
                other = g_ex[:, :, :].rearrange("p t (o e) -> p t o e", o=1).to_broadcast([P, TILES, NR, NR])
                own = g_ex[:, :, :].rearrange("p t (e o) -> p t e o", o=1).to_broadcast([P, TILES, NR, NR])
                four = lambda a: a.rearrange("p t (e f) -> p t e f", f=NR)
                eng.tensor_tensor(four(cmp_gt[:, :, :]), other, own, ALU.is_gt)
                link(eng.tensor_tensor(four(cmp_ge[:, :, :]), other, own, ALU.is_ge))
                link(eng.tensor_tensor(cmp_ge[:, :, :], cmp_ge[:, :, :], cmp_gt[:, :, :], ALU.subtract))
                low = lower[:, :, :].rearrange("p e (o f) -> p o (e f)", o=1).to_broadcast([P, TILES, NR * NR])
                link(eng.tensor_tensor(cmp_ge[:, :, :], cmp_ge[:, :, :], low, ALU.mult))
                link(eng.tensor_tensor(cmp_ge[:, :, :], cmp_ge[:, :, :], cmp_gt[:, :, :], ALU.add))
                eng.tensor_reduce(g_sum[:, 0, :], g_ex[:, :, :], AX.X, ALU.add)
                link(eng.tensor_reduce(rank[:, 0, :, :], four(cmp_ge[:, :, :]), AX.X, ALU.add))
                eng.reciprocal(g_sum[:, 1, :], g_sum[:, 0, :])
                link(eng.tensor_scalar(rank[:, 1, :, :], rank[:, 0, :, :], 2.0, None, ALU.is_lt))
                link(eng.tensor_tensor(rank[:, 2, :, :], rank[:, 1, :, :], g_ex[:, :, :], ALU.mult))
                eng.tensor_tensor(cw[:, :, :], rank[:, 2, :, :], per_tile(g_sum[:, 1, :]), ALU.mult)\
                   .then_inc(cw_ready, 1)

            def split_act(i, j):
                k = 4 * i + j
                for pair in range(2):
                    cols = slice(pair * 2 * HALF, (pair + 1) * 2 * HALF)
                    eng.wait_ge(gelu_done, FB * k + (2 * pair + 2))
                    after(eng, down_done, k - 1)
                    eng.tensor_copy(act_hi[:, j % 2, cols], act[:, j % 2, cols]).then_inc(act_rounded, 1)
                    eng.wait_ge(act_rounded, 2 * k + (pair + 1))
                    eng.tensor_tensor(act_lo[:, j % 2, cols], act[:, j % 2, cols],
                                      act_hi[:, j % 2, cols].bitcast(F32), ALU.subtract).then_inc(act_split, 1)

            def weigh(i, j):
                k = 4 * i + j
                s = j // 2
                eng.wait_ge(down_done, k + 1)
                eng.wait_ge(cwb_loaded[s], 16 * i + 16)
                after(eng, acc_done, k - 1)
                eng.scalar_tensor_tensor(out=part[:, j % 2, :], in0=banks[4 + j % 2][:, :],
                                         scalar=bias_now[:, s, FB:XB],
                                         in1=cwb[:, s, (j % 2) * HALF:(j % 2 + 1) * HALF],
                                         op0=ALU.add, op1=ALU.mult).then_inc(part_ready, 1)

            split_act(0, 0)
            router()

            def turn(i):
                for j in range(4):
                    if j < 3:
                        split_act(i, j + 1)
                    elif not isinstance(i, int) or i < NX // 2 - 1:
                        split_act(i + 1, 0)
                    weigh(i, j)
            turns(eng, turn)
            for q in range(2):
                eng.wait_ge(yT_done, q + 1)
                eng.tensor_tensor(y[:, 4 * q:4 * q + 4, :], banks[6 + q][:, :].rearrange("p (t d) -> p t d", d=P),
                                  h2[:, 4 * q:4 * q + 4, :], ALU.add).then_inc(y_ready, 1)

        @block.tensor
        def _(eng):
            def chunk(tile, parts, q, start, stop):
                for el in range(2):
                    c = (2 * q + el) * 512
                    mm = eng.matmul(banks[q][el * B:(el + 1) * B, :], tile[0:parts, WCOLS + P:TCOLS],
                                    tile[0:parts, c:c + 512], start=start, stop=stop)
                return mm

            eng.wait_ge(rest_masked, 1)
            for q in range(2):
                chunk(rest_tile, REST, q, True, False)
            with eng.Fori(0, LOOPS) as i:
                for r in range(RING):
                    eng.wait_ge(masked, RING * i + (r + 1))
                    for q in range(2):
                        mm = chunk(ring[:, r, :], P, q, False, False)
                    mm.then_inc(chunk_used, 1)
            for r in range(TAIL):
                for q in range(2):
                    last = r == TAIL - 1
                    eng.wait_ge(masked, RING * LOOPS + r + 1 + (q if last else 0))
                    mm = chunk(ring[:, r, :], P, q, False, last)
                    if last:
                        mm.then_inc(h_summed, 1)

            def transposes(dst, src, q, done):
                for n in range(4):
                    mm = eng.transpose(dst[:, n * P:(n + 1) * P], src(4 * q + n), ident[:, :])
                mm.then_inc(done, 1)

            eng.wait_ge(const_step, 4)
            for q in range(2):
                eng.wait_ge(h_added, q + 1)
                transposes(banks[2 + q], lambda t: h_rows[:, t, :], q, hT_done)
            eng.wait_ge(hT_copied[0], 2)
            eng.wait_ge(hT_copied[1], 2)
            for q in range(2):
                transposes(banks[4 + q], lambda t: h_cols[:, 8 * t:8 * t + 8, :], q, htok_done)
            for q in range(2):
                eng.wait_ge(xn_ready, 4 * q + 4)
                transposes(banks[6 + q], lambda t: xn[:, t, :], q, xnT_done)
            for q in range(2):
                eng.wait_ge(xnT_copied, q + 1)
                for n in range(4):
                    t = 4 * q + n
                    mm = eng.matmul(banks[q][:, n * P:(n + 1) * P], xn_cols[:, t, :], xn_cols[:, t, :],
                                    start=True, stop=True)
                mm.then_inc(gram_done, 1)
            eng.wait_ge(hn_ready, TILES)
            for q in range(2):
                eng.wait_ge(attn_ready, q + 1)
                for n in range(4):
                    t = 4 * q + n
                    eng.matmul(banks[2 + q][:, n * P:(n + 1) * P], attn[:, t, :], hn[:, t, :], start=True, stop=True)
                    mm = eng.matmul(banks[4 + q][:, n:n + 1], attn[:, t, :], ones[:, 0:1], start=True, stop=True)
                mm.then_inc(ctx_done, 1)
            for q in range(2):
                eng.wait_ge(t_ready, 4 * q + 4)
                transposes(banks[6 + q], lambda t: t_tok[:, t, :], q, tT_done)
            eng.wait_ge(gate_loaded, 32)
            for t in range(TILES):
                if t % 4 == 0:
                    eng.wait_ge(t_copied, t // 4 + 1)
                eng.matmul(banks[5][:, t * NR:(t + 1) * NR], t_cols[:, t * P:(t + 1) * P], gate_w_sb[:, :],
                           start=True, stop=False)
                mm = eng.matmul(banks[5][:, t * NR:(t + 1) * NR], ones[0:1, :], gate_b_sb[:, :],
                                start=False, stop=True)
            mm.then_inc(logits_done, 1)

            def up(i, j):
                k = 4 * i + j
                s, cols = (j // 2) % 2, slice((j % 2) * HALF, (j % 2 + 1) * HALF)
                if j % 2 == 0:
                    eng.wait_ge(w_split, 2 * i + (j // 2 + 1))
                if isinstance(k, int) and k < 2:
                    eng.wait_ge(t_split, k + 1)
                for fb in range(FB):
                    after(eng, gelu_done, FB * k + (fb + 1 - FB))
                    wh, wl = (w[:, s, fb * P:(fb + 1) * P] for w in (w_hi, w_lo))
                    eng.matmul(banks[fb][:, :], wh, t_hi[:, cols], start=True, stop=False)
                    eng.matmul(banks[fb][:, :], wh, t_lo[:, cols], start=False, stop=False)
                    eng.matmul(banks[fb][:, :], wl, t_hi[:, cols], start=False, stop=True).then_inc(up_done, 1)

            def down(i, j):
                k = 4 * i + j
                s = j // 2
                after(eng, part_ready, k - 1)
                for fb in range(FB):
                    if fb % 2 == 0:
                        eng.wait_ge(act_split, 2 * k + (fb // 2 + 1))
                    cols = slice(fb * HALF, (fb + 1) * HALF)
                    wh, wl = (w[:, s, FF + fb * P:FF + (fb + 1) * P] for w in (w_hi, w_lo))
                    o = banks[4 + j % 2][:, :]
                    eng.matmul(o, wh, act_hi[:, j % 2, cols], start=(fb == 0), stop=False)
                    eng.matmul(o, wh, act_lo[:, j % 2, cols], start=False, stop=False)
                    mm = eng.matmul(o, wl, act_hi[:, j % 2, cols], start=False, stop=(fb == FB - 1))
                mm.then_inc(down_done, 1)

            up(0, 0)

            def turn(i):
                for j in range(4):
                    if j < 3:
                        up(i, j + 1)
                    elif not isinstance(i, int) or i < NX // 2 - 1:
                        up(i + 1, 0)
                    if isinstance(i, int) and i == 0 and j == 0:
                        eng.wait_ge(cw_ready, 1)
                        for t in range(TILES):
                            mm = eng.transpose(banks[6 + t // 4][0:NR, (t % 4) * P:(t % 4 + 1) * P], cw[:, t, :],
                                               ident[:, :])
                            if t % 4 == 3:
                                mm.then_inc(cwT_done, 1)
                    down(i, j)
            turns(eng, turn)
            eng.wait_ge(cw_copied, 2)
            for q in range(2):
                eng.wait_ge(acc_done, 2 * NX - 1 + q)
                transposes(banks[6 + q], lambda t: acc[:, t * P:(t + 1) * P], q, yT_done)


def kernel(x, L0_tok_weight, L0_tok_bias, L0_tok_mask, L0_ffn_gate_w, L0_ffn_gate_b, L0_ffn_sw1, L0_ffn_sb1,
           L0_ffn_sw2, L0_ffn_sb2, L0_ffn_rw1, L0_ffn_rb1, L0_ffn_rw2, L0_ffn_rb2):
    import numpy as np
    import concourse.bacc as bacc
    from concourse.bass_utils import run_bass_kernel_spmd

    c = np.ascontiguousarray
    weight = np.asarray(L0_tok_weight)
    order = [e for q in range(2) for el in range(2) for e in range(8 * el + 4 * q, 8 * el + 4 * q + 4)]
    rows = np.concatenate([weight[order].transpose(1, 0, 2).reshape(G, WCOLS), np.asarray(L0_tok_mask),
                           np.asarray(x).T], axis=1)
    w1 = np.concatenate([np.asarray(L0_ffn_sw1), np.asarray(L0_ffn_rw1)])
    w2 = np.concatenate([np.asarray(L0_ffn_sw2), np.asarray(L0_ffn_rw2)])
    b1 = np.concatenate([np.asarray(L0_ffn_sb1), np.asarray(L0_ffn_rb1)])
    b2 = np.concatenate([np.asarray(L0_ffn_sb2), np.asarray(L0_ffn_rb2)])
    w2t = w2.transpose(0, 2, 1).reshape(NX, FB, P, P).transpose(0, 2, 1, 3).reshape(NX, P, FB * P)
    arrays = {
        "tiles": c(rows[:CHUNKS * P].reshape(CHUNKS, P, TCOLS)),
        "rest": c(rows[CHUNKS * P:]),
        "tok_bias": c(np.asarray(L0_tok_bias).reshape(2, E // 2 * P)),
        "experts": c(np.concatenate([w1.transpose(0, 2, 1), w2t, b1.reshape(NX, FB, P).transpose(0, 2, 1),
                                     b2[:, :, None]], axis=2)),
        "gate_w": c(np.asarray(L0_ffn_gate_w).T),
        "gate_b": c(np.asarray(L0_ffn_gate_b).reshape(1, NR)),
    }
    nc = bacc.Bacc("TRN2", target_bir_lowering=False, num_devices=1)
    args = [nc.dram_tensor(f"{n}_dram", a.shape, F32, kind="ExternalInput").ap() for n, a in arrays.items()]
    args.append(nc.dram_tensor("out_dram", (TOK, P), F32, kind="ExternalOutput").ap())
    build(nc, *args)
    r = run_bass_kernel_spmd(nc, [{f"{n}_dram": a for n, a in arrays.items()}], core_ids=[0])
    return r.results[0]["out_dram"].reshape(B, E, P)
```

```python
import concourse.bass as bass
from concourse import mybir
from contextlib import ExitStack

F32 = mybir.dt.float32
F32R = mybir.dt.float32r
ALU = mybir.AluOpType
ACT = mybir.ActivationFunctionType
AX = mybir.AxisListType

P = 128
B, E, G = 64, 16, 5000
CHUNKS = G // P
REST = G - CHUNKS * P + 1
WCOLS = E * P
W0 = P + B
TCOLS = W0 + WCOLS
RING = 6
LOOPS = CHUNKS // RING
TAIL = CHUNKS - LOOPS * RING
TOK = B * E
TILES = TOK // P
HALF = TOK // 2
NS, NR = 2, 8
NX = NS + NR
FF = 512
FB = FF // P
WX = FF + FB * P
XB = FB + 1
LN_EPS = 1e-05
NORM_EPS = 1e-12


def build(nc, tiles, rest, experts, gate_w, gate_b, out):
    ctx = ExitStack()
    with ctx:
        def sb(name, shape, dt=F32):
            return ctx.enter_context(nc.sbuf_tensor(name, shape, dt))

        def sem(name):
            return ctx.enter_context(nc.semaphore(name))

        ring = sb("ring", [P, RING, TCOLS])
        rest_tile = sb("rest_tile", [REST, TCOLS])
        ident = sb("ident", [P, P])
        block_mask = sb("block_mask", [P, P])
        lower = sb("lower", [P, NR, NR])
        ones = sb("ones", [P, P])
        gate_w_sb = sb("gate_w_sb", [P, NR])
        gate_hi = sb("gate_hi", [P, NR], F32R)
        gate_lo = sb("gate_lo", [P, NR], F32R)
        gate_b_sb = sb("gate_b_sb", [NR, 1])
        logit_rows = sb("logit_rows", [NR, TOK])
        zeros = sb("zeros", [P, XB])
        h_rows = sb("h_rows", [P, TILES, P])
        h_cols = sb("h_cols", [P, B, E])
        h_tok = sb("h_tok", [P, TILES, P])
        hn = sb("hn", [P, TILES, P + 1])
        xn = sb("xn", [P, TILES, P])
        xn_cols = sb("xn_cols", [P, TILES, P])
        sq = sb("sq", [P, TILES, P])
        ex = sb("ex", [P, TILES, P])
        attn = sb("attn", [P, TILES, P])
        h2 = sb("h2", [P, TILES, P])
        t_tok = h_rows
        t_hi = sb("t_hi", [P, TOK], F32R)
        t_lo = sb("t_lo", [P, TOK], F32R)
        stats = sb("stats", [P, 2, TILES, 6])
        mv = sb("mv", [P, 2, TILES, 2])
        base = sb("base", [P, 3, TILES])
        root = sb("root", [P, 4, TILES])
        small = sb("small", [P, 6, TILES])
        g_max = sb("g_max", [P, TILES])
        g_sh = sb("g_sh", [P, TILES, NR])
        g_ex = sb("g_ex", [P, TILES, NR])
        g_sum = sb("g_sum", [P, 2, TILES])
        cmp_ge = sb("cmp_ge", [P, TILES, NR * NR])
        cmp_gt = sb("cmp_gt", [P, TILES, NR * NR])
        rank = sb("rank", [P, 3, TILES, NR])
        cw = sb("cw", [P, TILES, NR])
        cw_cols = sb("cw_cols", [NR, TOK])
        one_rows = sb("one_rows", [NS, TOK])
        cw_dram = nc.dram_tensor("cw_dram", [NX, TOK], F32, kind="Internal").ap()
        w_raw = sb("w_raw", [P, 2, WX + XB])
        bias_now = sb("bias_now", [P, 2, XB])
        w_hi = sb("w_hi", [P, 2, WX], F32R)
        w_lo = sb("w_lo", [P, 2, WX], F32R)
        over = ring[:, :, :].rearrange("p r c -> p (r c)")
        act = over[:, 0:2 * FB * HALF].rearrange("p (s c) -> p s c", s=2)
        act_hi = sb("act_hi", [P, 2, FB * HALF], F32R)
        act_lo = sb("act_lo", [P, 2, FB * HALF], F32R)
        cwb = over[:, 2 * FB * HALF:2 * FB * HALF + 2 * TOK].rearrange("p (s c) -> p s c", s=2)
        part = sb("part", [P, 2, HALF])
        acc = sb("acc", [P, TOK])
        y = sb("y", [P, TILES, P])

        psum = ctx.enter_context(nc.psum_tensor("psum", [P, 8, 512], F32))
        banks = [psum[:, n, :] for n in range(8)]

        tile_loaded = [sem(f"tile_loaded{r}") for r in range(RING)]
        last_loaded = sem("last_loaded")
        rest_loaded = sem("rest_loaded")
        rest_masked = sem("rest_masked")
        masked = sem("masked")
        chunk_used = sem("chunk_used")
        h_summed = sem("h_summed")
        gate_loaded = sem("gate_loaded")
        const_step = sem("const_step")
        h_evacuated = [sem("h_evacuated0"), sem("h_evacuated1")]
        hT_done = sem("hT_done")
        hT_copied = [sem("hT_copied0"), sem("hT_copied1")]
        htok_done = sem("htok_done")
        htok_copied = sem("htok_copied")
        dve_link = sem("dve_link")
        base_ready = sem("base_ready")
        root_ready = sem("root_ready")
        scales_ready = sem("scales_ready")
        hn_ready = sem("hn_ready")
        xn_ready = [sem("xn_ready0"), sem("xn_ready1")]
        xnT_done = sem("xnT_done")
        xnT_copied = sem("xnT_copied")
        gram_done = sem("gram_done")
        sq_done = sem("sq_done")
        ex_done = sem("ex_done")
        attn_ready = sem("attn_ready")
        ctx_done = sem("ctx_done")
        t_ready = [sem("t_ready0"), sem("t_ready1")]
        tT_done = sem("tT_done")
        t_rounded = sem("t_rounded")
        t_split = sem("t_split")
        gate_rounded = sem("gate_rounded")
        gate_split = sem("gate_split")
        gate_done = sem("gate_done")
        logits_copied = sem("logits_copied")
        logits_done = sem("logits_done")
        g_shifted = sem("g_shifted")
        g_exped = sem("g_exped")
        cw_ready = sem("cw_ready")
        cwT_done = sem("cwT_done")
        cw_copied = sem("cw_copied")
        cw_stored = sem("cw_stored")
        w_loaded = [sem("w_loaded0"), sem("w_loaded1")]
        w_rounded = sem("w_rounded")
        w_split = sem("w_split")
        cwb_loaded = [sem("cwb_loaded0"), sem("cwb_loaded1")]
        up_done = sem("up_done")
        gelu_done = sem("gelu_done")
        act_rounded = [sem("act_rounded0"), sem("act_rounded1")]
        act_split = sem("act_split")
        down_done = sem("down_done")
        part_ready = sem("part_ready")
        acc_done = sem("acc_done")
        yT_done = sem("yT_done")
        y_ready = sem("y_ready")
        out_stored = sem("out_stored")

        block = ctx.enter_context(nc.Block())

        def after(eng, s, value):
            if not isinstance(value, int) or value > 0:
                eng.wait_ge(s, value)

        def turns(eng, body):
            body(0)
            with eng.Fori(1, NX // 2 - 1) as i:
                body(i)
            body(NX // 2 - 1)

        @block.sync
        def _(eng):
            eng.dma_start(rest_tile[:, :], rest).then_inc(rest_loaded, 16)
            for r in range(RING):
                eng.dma_start(ring[:, r, :], tiles[r]).then_inc(tile_loaded[r], 16)
            with eng.Fori(1, LOOPS) as i:
                for r in range(RING):
                    eng.wait_ge(chunk_used, RING * i + (r + 1 - RING))
                    eng.dma_start(ring[:, r, :], tiles[bass.ds(RING * i + r, 1)].rearrange("a p c -> (a p) c"))\
                       .then_inc(tile_loaded[r], 16)
            for r in range(TAIL):
                eng.wait_ge(chunk_used, RING * (LOOPS - 1) + r + 1)
                if r < TAIL - 1:
                    eng.dma_start(ring[:, r, :], tiles[RING * LOOPS + r]).then_inc(tile_loaded[r], 16)
                else:
                    cut = W0 + WCOLS // 2
                    eng.dma_start(ring[:, r, 0:cut], tiles[CHUNKS - 1, :, 0:cut]).then_inc(tile_loaded[r], 16)
                    eng.dma_start(ring[:, r, cut:], tiles[CHUNKS - 1, :, cut:]).then_inc(last_loaded, 16)
            for x in range(2):
                eng.dma_start(w_raw[:, x, :], experts[x]).then_inc(w_loaded[x], 16)
            eng.wait_ge(const_step, 1)
            eng.dma_start(cw_dram[0:NS, :], one_rows[:, :]).then_inc(cw_stored, 16)
            eng.wait_ge(cw_stored, 16)
            eng.wait_ge(h_summed, 2)

            def turn(i):
                for s in range(2):
                    x = 2 * i + s
                    after(eng, part_ready, 2 * x - 2)
                    eng.dma_start(cwb[:, s, :], cw_dram[bass.ds(x, 1), :].to_broadcast([P, TOK]))\
                       .then_inc(cwb_loaded[s], 16)
                    if not isinstance(i, int) or i < NX // 2 - 1:
                        eng.wait_ge(w_split, 2 * x + 2)
                        eng.dma_start(w_raw[:, s, :], experts[bass.ds(x + 2, 1)].rearrange("a p c -> (a p) c"))\
                           .then_inc(w_loaded[s], 16)
                if isinstance(i, int) and i == 0:
                    eng.wait_ge(cw_copied, 2)
                    eng.dma_start(cw_dram[NS:NX, :], cw_cols[:, :]).then_inc(cw_stored, 16)
                    eng.wait_ge(cw_stored, 32)
            turns(eng, turn)
            for q in range(2):
                eng.wait_ge(y_ready, q + 1)
                eng.dma_start(out.rearrange("(t p) d -> p t d", p=P)[:, 4 * q:4 * q + 4, :],
                              y[:, 4 * q:4 * q + 4, :]).then_inc(out_stored, 16)
            eng.wait_ge(out_stored, 32)

        @block.gpsimd
        def _(eng):
            eng.memset(one_rows[:, :], 1.0).then_inc(const_step, 1)
            eng.memset(ident[:, :], 0.0)
            eng.memset(block_mask[:, :], 1.0)
            eng.memset(lower[:, :, :], 1.0)
            eng.memset(ones[:, :], 1.0)
            eng.memset(hn[:, :, P:P + 1], 1.0)
            eng.memset(zeros[:, :], 0.0)
            eng.memset(acc[:, :], 0.0).then_inc(const_step, 1)
            eng.wait_ge(const_step, 2)
            eng.affine_select(out=ident[:, :], in_=ident[:, :], compare_op=ALU.not_equal, fill=1.0,
                              base=0, pattern=[[-1, P]], channel_multiplier=1)
            bm = block_mask[:, :].rearrange("p (n e) -> p n e", e=E)
            eng.affine_select(out=bm, in_=bm, compare_op=ALU.is_ge, fill=0.0, base=0,
                              pattern=[[-E, P // E], [0, E]], channel_multiplier=1).then_inc(const_step, 1)
            eng.affine_select(out=lower[:, :, :], in_=lower[:, :, :], compare_op=ALU.is_gt, fill=0.0, base=0,
                              pattern=[[1, NR], [-1, NR]], channel_multiplier=0)
            eng.wait_ge(const_step, 3)
            eng.affine_select(out=bm, in_=bm, compare_op=ALU.is_ge, fill=0.0, base=E - 1,
                              pattern=[[E, P // E], [0, E]], channel_multiplier=-1).then_inc(const_step, 1)

            def low_parts(part, s, x):
                eng.wait_ge(w_rounded, 2 * x + (part + 1))
                b, cols = (slice(0, FB), slice(FB, XB))[part], slice(part * FF, (part + 1) * FF)
                eng.tensor_tensor(bias_now[:, s, b], w_raw[:, s, WX + b.start:WX + b.stop], zeros[:, b], ALU.add)
                eng.tensor_tensor(w_lo[:, s, cols], w_raw[:, s, cols], w_hi[:, s, cols].bitcast(F32), ALU.subtract)\
                   .then_inc(w_split, 1)

            eng.wait_ge(gate_rounded, 1)
            eng.tensor_tensor(gate_lo[:, :], gate_w_sb[:, :], gate_hi[:, :].bitcast(F32), ALU.subtract)\
               .then_inc(gate_split, 1)
            for x in range(2):
                for m in range(2):
                    low_parts(m, x, x)

            def turn(i):
                more = not isinstance(i, int) or i < NX // 2 - 1
                for j in range(4):
                    k = 4 * i + j
                    if j % 2 == 0 and more:
                        eng.wait_ge(gelu_done, FB * (k + 2))
                        low_parts(0, j // 2, 2 * i + (j // 2 + 2))
                    eng.wait_ge(part_ready, k + 1)
                    after(eng, acc_done, k - 1)
                    half = acc[:, (j % 2) * HALF:(j % 2 + 1) * HALF]
                    eng.tensor_tensor(half, half, part[:, j % 2, :], ALU.add).then_inc(acc_done, 1)
                    if j % 2 and more:
                        low_parts(1, j // 2, 2 * i + (j // 2 + 2))
            turns(eng, turn)

        @block.scalar
        def _(eng):
            eng.dma_start(gate_w_sb[:, :], gate_w).then_inc(gate_loaded, 16)
            eng.dma_start(gate_b_sb[:, :], gate_b).then_inc(gate_loaded, 16)
            eng.wait_ge(const_step, 2)
            eng.activation(root[:, 3, 0:1], ones[:, 0:1], ACT.Sqrt)
            eng.wait_ge(gate_loaded, 32)
            eng.activation(gate_hi[:, :], gate_w_sb[:, :], ACT.Copy).then_inc(gate_rounded, 1)
            tiled = lambda a: a.rearrange("p (t d) -> p t d", d=P)
            eng.wait_ge(h_summed, 2)
            eng.activation(h_rows[:, 4:8, :], tiled(banks[1][:, :]), ACT.Copy).then_inc(h_evacuated[1], 1)
            eng.wait_ge(hT_done, 1)
            for el in range(2):
                eng.activation(h_cols[:, :, el * 8:el * 8 + 4],
                               banks[2][:, :].rearrange("p (h l b) -> p l b h", h=4, l=2)[:, el],
                               ACT.Copy).then_inc(hT_copied[0], 1)
            for q in range(2):
                eng.wait_ge(htok_done, q + 1)
                eng.activation(h_tok[:, 4 * q:4 * q + 4, :], tiled(banks[4 + q][:, :]), ACT.Copy)\
                   .then_inc(htok_copied, 1)
            eng.wait_ge(base_ready, 1)
            eng.activation(root[:, 0:2, :], base[:, 0:2, :], ACT.Sqrt).then_inc(root_ready, 1)
            eng.wait_ge(scales_ready, 1)
            for t in range(4, 8):
                n = eng.activation(xn[:, t, :], h_tok[:, t, :], ACT.Identity, scale=small[:, 2, t:t + 1],
                                   bias=small[:, 3, t:t + 1])
            n.then_inc(xn_ready[1], 1)
            for q in range(2):
                eng.wait_ge(xnT_done, q + 1)
                eng.activation(xn_cols[:, 4 * q:4 * q + 4, :], tiled(banks[6 + q][:, :]), ACT.Copy)\
                   .then_inc(xnT_copied, 1)
            eng.activation(root[:, 3, 2:3], ones[:, 0:1], ACT.Exp)
            for q in range(2):
                eng.wait_ge(gram_done, q + 1)
                eng.activation(sq[:, 4 * q:4 * q + 4, :], tiled(banks[q][:, :]), ACT.Square).then_inc(sq_done, 1)
                eng.wait_ge(sq_done, q + 1)
                eng.activation(ex[:, 4 * q:4 * q + 4, :], sq[:, 4 * q:4 * q + 4, :], ACT.Exp).then_inc(ex_done, 1)

            def high_parts(part, s, x):
                cols = slice(part * FF, (part + 1) * FF)
                if part == 0:
                    eng.wait_ge(w_loaded[s], 8 * (x - s) + 16 if isinstance(x, int) else 8 * x + (16 - 8 * s))
                    after(eng, gelu_done, 2 * FB * (x - 1))
                else:
                    after(eng, down_done, 2 * (x - 1))
                eng.activation(w_hi[:, s, cols], w_raw[:, s, cols], ACT.Copy).then_inc(w_rounded, 1)

            eng.activation(root[:, 3, 1:2], ones[:, 0:1], ACT.Sqrt)
            for x in range(2):
                for m in range(2):
                    high_parts(m, x, x)
            eng.wait_ge(base_ready, 2)
            eng.activation(root[:, 2, :], base[:, 2, :], ACT.Sqrt).then_inc(root_ready, 1)
            eng.wait_ge(scales_ready, 2)
            for t in range(4, 8):
                n = eng.activation(t_tok[:, t, :], h2[:, t, :], ACT.Identity, scale=small[:, 4, t:t + 1],
                                   bias=small[:, 5, t:t + 1])
            n.then_inc(t_ready[1], 1)
            for q in range(2):
                eng.wait_ge(tT_done, q + 1)
                eng.activation(t_hi[:, q * HALF:(q + 1) * HALF], banks[6 + q][:, :], ACT.Copy).then_inc(t_rounded, 1)

            def gelu(i, j):
                k = 4 * i + j
                after(eng, act_split, 2 * k - 2)
                for fb in range(FB):
                    eng.wait_ge(up_done, FB * k + (fb + 1))
                    eng.activation(act[:, j % 2, fb * HALF:(fb + 1) * HALF], banks[fb][:, :], ACT.Gelu,
                                   bias=bias_now[:, j // 2, fb:fb + 1]).then_inc(gelu_done, 1)
                after(eng, down_done, k - 1)
                eng.wait_ge(gelu_done, FB * k + FB)
                eng.activation(act_hi[:, j % 2, 2 * HALF:], act[:, j % 2, 2 * HALF:], ACT.Copy)\
                   .then_inc(act_rounded[1], 1)

            def turn(i):
                first = isinstance(i, int) and i == 0
                last = isinstance(i, int) and i == NX // 2 - 1
                for j in range(4):
                    gelu(i, j)
                    if first and j == 0:
                        for q in range(2):
                            eng.wait_ge(gate_done, q + 1)
                            eng.activation(logit_rows[:, q * HALF:(q + 1) * HALF], banks[6 + q][0:NR, :],
                                           ACT.Identity, bias=gate_b_sb[:, :]).then_inc(logits_copied, 1)
                    if first and j == 1:
                        eng.wait_ge(g_shifted, 1)
                        eng.activation(g_ex[:, :, :], g_sh[:, :, :], ACT.Exp).then_inc(g_exped, 1)
                    if j % 2 and not last:
                        high_parts(0, j // 2, 2 * i + (j // 2 + 2))
                    if j == 2 and not last:
                        high_parts(1, 0, 2 * i + 2)
                    if j == 0 and not first:
                        high_parts(1, 1, 2 * i + 1)
                    if first and j == 2:
                        for q in range(2):
                            eng.wait_ge(cwT_done, q + 1)
                            eng.activation(cw_cols[:, q * HALF:(q + 1) * HALF], banks[6 + q][0:NR, :], ACT.Copy)\
                               .then_inc(cw_copied, 1)
            turns(eng, turn)

        @block.vector
        def _(eng):
            links = [0]

            def link(ins):
                links[0] += 1
                ins.then_inc(dve_link, 1)
                eng.wait_ge(dve_link, links[0])

            def apply_mask(tile, parts, e0, e1):
                w = tile[:, W0 + e0 * P:W0 + e1 * P].rearrange("p (e d) -> p e d", d=P)
                m = tile[:, 0:P].rearrange("p (o d) -> p o d", o=1).to_broadcast([parts, e1 - e0, P])
                return eng.tensor_tensor(w, w, m, ALU.mult)

            eng.wait_ge(rest_loaded, 16)
            apply_mask(rest_tile, REST, 0, E).then_inc(rest_masked, 1)
            with eng.Fori(0, LOOPS) as i:
                for r in range(RING):
                    eng.wait_ge(tile_loaded[r], 16 * i + 16)
                    apply_mask(ring[:, r, :], P, 0, E).then_inc(masked, 1)
            for r in range(TAIL):
                eng.wait_ge(tile_loaded[r], 16 * LOOPS + 16)
                if r < TAIL - 1:
                    apply_mask(ring[:, r, :], P, 0, E).then_inc(masked, 1)
                else:
                    for q in range(2):
                        if q:
                            eng.wait_ge(last_loaded, 16)
                        apply_mask(ring[:, r, :], P, 8 * q, 8 * q + 8).then_inc(masked, 1)

            eng.wait_ge(h_summed, 1)
            eng.tensor_copy(h_rows[:, 0:4, :], banks[0][:, :].rearrange("p (t d) -> p t d", d=P))\
               .then_inc(h_evacuated[0], 1)
            eng.wait_ge(hT_done, 2)
            for el in range(2):
                eng.tensor_copy(h_cols[:, :, el * 8 + 4:el * 8 + 8],
                                banks[3][:, :].rearrange("p (h l b) -> p l b h", h=4, l=2)[:, el])\
                   .then_inc(hT_copied[1], 1)

            def norm_aggregate(n):
                for t in range(TILES):
                    a = eng.bn_aggr(mv[:, n, t, :], stats[:, n, t, :])
                link(a)

            for t in range(TILES):
                if t % 4 == 0:
                    eng.wait_ge(htok_copied, t // 4 + 1)
                s = eng.bn_stats(stats[:, 0, t, :], h_tok[:, t, :])
            link(s)
            norm_aggregate(0)
            eng.tensor_scalar(base[:, 0, :], mv[:, 0, :, 1], LN_EPS, None, ALU.add)
            eng.tensor_scalar(base[:, 1, :], mv[:, 0, :, 1], float(P), None, ALU.mult).then_inc(base_ready, 1)
            eng.wait_ge(root_ready, 1)
            link(eng.scalar_tensor_tensor(out=small[:, 0, :], in0=root[:, 0, :], scalar=NORM_EPS, in1=root[:, 1, :],
                                          op0=ALU.mult, op1=ALU.add))
            link(eng.reciprocal(small[:, 2, :], small[:, 0, :]))
            eng.scalar_tensor_tensor(out=small[:, 3, :], in0=mv[:, 0, :, 0], scalar=-1.0, in1=small[:, 2, :],
                                     op0=ALU.mult, op1=ALU.mult).then_inc(scales_ready, 1)
            for t in range(4):
                s = eng.tensor_scalar(xn[:, t, :], h_tok[:, t, :], mv[:, 0, t, 0:1], small[:, 2, t:t + 1],
                                      ALU.subtract, ALU.mult)
            s.then_inc(xn_ready[0], 1)
            link(eng.reciprocal(small[:, 1, :], root[:, 0, :]))
            for t in range(TILES):
                s = eng.tensor_scalar(hn[:, t, 0:P], h_tok[:, t, :], mv[:, 0, t, 0:1], small[:, 1, t:t + 1],
                                      ALU.subtract, ALU.mult)
            s.then_inc(hn_ready, 1)
            eng.wait_ge(const_step, 4)
            for q in range(2):
                eng.wait_ge(ex_done, q + 1)
                m = block_mask[:, :].rearrange("p (o d) -> p o d", o=1).to_broadcast([P, 4, P])
                eng.tensor_tensor(attn[:, 4 * q:4 * q + 4, :], ex[:, 4 * q:4 * q + 4, :], m, ALU.mult)\
                   .then_inc(attn_ready, 1)
            for q in range(2):
                eng.wait_ge(ctx_done, q + 1)
                link(eng.reciprocal(g_sum[:, 0, 4 * q:4 * q + 4].rearrange("p (a b) -> p a b", b=2),
                                    psum[:, 2 + 2 * q:4 + 2 * q, P:2 * P + 2:P + 1]))
                for t in range(4 * q, 4 * q + 4):
                    c = (t % 2) * (P + 1)
                    s = eng.scalar_tensor_tensor(out=h2[:, t, :], in0=banks[2 + t // 2][:, c:c + P],
                                                 scalar=g_sum[:, 0, t:t + 1], in1=h_tok[:, t, :],
                                                 op0=ALU.mult, op1=ALU.add)
                link(s)
                for t in range(4 * q, 4 * q + 4):
                    s = eng.bn_stats(stats[:, 1, t, :], h2[:, t, :])
            link(s)
            norm_aggregate(1)
            eng.tensor_scalar(base[:, 2, :], mv[:, 1, :, 1], LN_EPS, None, ALU.add).then_inc(base_ready, 1)
            eng.wait_ge(root_ready, 2)
            link(eng.reciprocal(small[:, 4, :], root[:, 2, :]))
            eng.scalar_tensor_tensor(out=small[:, 5, :], in0=mv[:, 1, :, 0], scalar=-1.0, in1=small[:, 4, :],
                                     op0=ALU.mult, op1=ALU.mult).then_inc(scales_ready, 1)
            for t in range(4):
                s = eng.tensor_scalar(t_tok[:, t, :], h2[:, t, :], mv[:, 1, t, 0:1], small[:, 4, t:t + 1],
                                      ALU.subtract, ALU.mult)
            s.then_inc(t_ready[0], 1)
            for q in range(2):
                cols = slice(q * HALF, (q + 1) * HALF)
                eng.wait_ge(t_rounded, q + 1)
                eng.tensor_tensor(t_lo[:, cols], banks[6 + q][:, :], t_hi[:, cols].bitcast(F32), ALU.subtract)\
                   .then_inc(t_split, 1)

            per_tile = lambda a: a.rearrange("p (t o) -> p t o", o=1).to_broadcast([P, TILES, NR])

            def router_shift():
                eng.wait_ge(logits_done, 1)
                logits = banks[6][:, 0:TILES * NR].rearrange("p (t e) -> p t e", e=NR)
                link(eng.tensor_reduce(g_max[:, :], logits, AX.X, ALU.max))
                eng.tensor_tensor(g_sh[:, :, :], logits, per_tile(g_max[:, :]), ALU.subtract).then_inc(g_shifted, 1)

            def router():
                eng.wait_ge(g_exped, 1)
                other = g_ex[:, :, :].rearrange("p t (o e) -> p t o e", o=1).to_broadcast([P, TILES, NR, NR])
                own = g_ex[:, :, :].rearrange("p t (e o) -> p t e o", o=1).to_broadcast([P, TILES, NR, NR])
                four = lambda a: a.rearrange("p t (e f) -> p t e f", f=NR)
                eng.tensor_tensor(four(cmp_gt[:, :, :]), other, own, ALU.is_gt)
                link(eng.tensor_tensor(four(cmp_ge[:, :, :]), other, own, ALU.is_ge))
                link(eng.tensor_tensor(cmp_ge[:, :, :], cmp_ge[:, :, :], cmp_gt[:, :, :], ALU.subtract))
                low = lower[:, :, :].rearrange("p e (o f) -> p o (e f)", o=1).to_broadcast([P, TILES, NR * NR])
                link(eng.tensor_tensor(cmp_ge[:, :, :], cmp_ge[:, :, :], low, ALU.mult))
                link(eng.tensor_tensor(cmp_ge[:, :, :], cmp_ge[:, :, :], cmp_gt[:, :, :], ALU.add))
                eng.tensor_reduce(g_sum[:, 0, :], g_ex[:, :, :], AX.X, ALU.add)
                link(eng.tensor_reduce(rank[:, 0, :, :], four(cmp_ge[:, :, :]), AX.X, ALU.add))
                eng.reciprocal(g_sum[:, 1, :], g_sum[:, 0, :])
                link(eng.tensor_scalar(rank[:, 1, :, :], rank[:, 0, :, :], 2.0, None, ALU.is_lt))
                link(eng.tensor_tensor(rank[:, 2, :, :], rank[:, 1, :, :], g_ex[:, :, :], ALU.mult))
                eng.tensor_tensor(cw[:, :, :], rank[:, 2, :, :], per_tile(g_sum[:, 1, :]), ALU.mult)\
                   .then_inc(cw_ready, 1)

            def split_act(i, j):
                k = 4 * i + j
                eng.wait_ge(gelu_done, FB * k + 2)
                after(eng, down_done, k - 1)
                first, second = slice(0, 2 * HALF), slice(2 * HALF, 4 * HALF)
                eng.tensor_copy(act_hi[:, j % 2, first], act[:, j % 2, first]).then_inc(act_rounded[0], 1)
                for rounded, cols in zip(act_rounded, (first, second)):
                    eng.wait_ge(rounded, k + 1)
                    eng.tensor_tensor(act_lo[:, j % 2, cols], act[:, j % 2, cols],
                                      act_hi[:, j % 2, cols].bitcast(F32), ALU.subtract).then_inc(act_split, 1)

            def weigh(i, j):
                k = 4 * i + j
                s = j // 2
                eng.wait_ge(down_done, k + 1)
                eng.wait_ge(cwb_loaded[s], 16 * i + 16)
                after(eng, acc_done, k - 1)
                eng.scalar_tensor_tensor(out=part[:, j % 2, :], in0=banks[4 + j % 2][:, :],
                                         scalar=bias_now[:, s, FB:XB],
                                         in1=cwb[:, s, (j % 2) * HALF:(j % 2 + 1) * HALF],
                                         op0=ALU.add, op1=ALU.mult).then_inc(part_ready, 1)

            split_act(0, 0)
            router_shift()

            def turn(i):
                for j in range(4):
                    if isinstance(i, int) and i == 0 and j == 1:
                        router()
                    if j < 3:
                        split_act(i, j + 1)
                    elif not isinstance(i, int) or i < NX // 2 - 1:
                        split_act(i + 1, 0)
                    weigh(i, j)
            turns(eng, turn)
            for q in range(2):
                eng.wait_ge(yT_done, q + 1)
                eng.tensor_tensor(y[:, 4 * q:4 * q + 4, :], banks[6 + q][:, :].rearrange("p (t d) -> p t d", d=P),
                                  h2[:, 4 * q:4 * q + 4, :], ALU.add).then_inc(y_ready, 1)

        @block.tensor
        def _(eng):
            def chunk(tile, parts, q, start, stop):
                for el in range(2):
                    c = W0 + (2 * q + el) * 512
                    mm = eng.matmul(banks[q][el * B:(el + 1) * B, :], tile[0:parts, P:W0],
                                    tile[0:parts, c:c + 512], start=start, stop=stop)
                return mm

            eng.wait_ge(rest_masked, 1)
            for q in range(2):
                chunk(rest_tile, REST, q, True, False)
            with eng.Fori(0, LOOPS) as i:
                for r in range(RING):
                    eng.wait_ge(masked, RING * i + (r + 1))
                    for q in range(2):
                        mm = chunk(ring[:, r, :], P, q, False, False)
                    mm.then_inc(chunk_used, 1)
            for r in range(TAIL):
                for q in range(2):
                    last = r == TAIL - 1
                    eng.wait_ge(masked, RING * LOOPS + r + 1 + (q if last else 0))
                    mm = chunk(ring[:, r, :], P, q, False, last)
                    if last:
                        mm.then_inc(h_summed, 1)

            def transposes(dst, src, q, done):
                for n in range(4):
                    mm = eng.transpose(dst[:, n * P:(n + 1) * P], src(4 * q + n), ident[:, :])
                mm.then_inc(done, 1)

            eng.wait_ge(const_step, 4)
            for q in range(2):
                eng.wait_ge(h_evacuated[q], 1)
                transposes(banks[2 + q], lambda t: h_rows[:, t, :], q, hT_done)
            eng.wait_ge(hT_copied[0], 2)
            eng.wait_ge(hT_copied[1], 2)
            for q in range(2):
                transposes(banks[4 + q], lambda t: h_cols[:, 8 * t:8 * t + 8, :], q, htok_done)
            for q in range(2):
                eng.wait_ge(xn_ready[q], 1)
                transposes(banks[6 + q], lambda t: xn[:, t, :], q, xnT_done)
            for q in range(2):
                eng.wait_ge(xnT_copied, q + 1)
                for n in range(4):
                    t = 4 * q + n
                    mm = eng.matmul(banks[q][:, n * P:(n + 1) * P], xn_cols[:, t, :], xn_cols[:, t, :],
                                    start=True, stop=True)
                mm.then_inc(gram_done, 1)
            eng.wait_ge(hn_ready, 1)
            for q in range(2):
                eng.wait_ge(attn_ready, q + 1)
                for n in range(4):
                    t = 4 * q + n
                    c = (t % 2) * (P + 1)
                    mm = eng.matmul(banks[2 + t // 2][:, c:c + P + 1], attn[:, t, :], hn[:, t, :],
                                    start=True, stop=True)
                mm.then_inc(ctx_done, 1)
            for q in range(2):
                eng.wait_ge(t_ready[q], 1)
                transposes(banks[6 + q], lambda t: t_tok[:, t, :], q, tT_done)
            def up(i, j):
                k = 4 * i + j
                s, cols = (j // 2) % 2, slice((j % 2) * HALF, (j % 2 + 1) * HALF)
                if j % 2 == 0:
                    eng.wait_ge(w_split, 4 * i + (j + 1))
                if isinstance(k, int) and k < 2:
                    eng.wait_ge(t_split, k + 1)
                for fb in range(FB):
                    after(eng, gelu_done, FB * k + (fb + 1 - FB))
                    wh, wl = (w[:, s, fb * P:(fb + 1) * P] for w in (w_hi, w_lo))
                    eng.matmul(banks[fb][:, :], wh, t_hi[:, cols], start=True, stop=False)
                    eng.matmul(banks[fb][:, :], wh, t_lo[:, cols], start=False, stop=False)
                    eng.matmul(banks[fb][:, :], wl, t_hi[:, cols], start=False, stop=True).then_inc(up_done, 1)

            def down(i, j):
                k = 4 * i + j
                s = j // 2
                if j % 2 == 0:
                    eng.wait_ge(w_split, 4 * i + (j + 2))
                after(eng, part_ready, k - 1)
                for fb in range(FB):
                    if fb % 2 == 0:
                        eng.wait_ge(act_split, 2 * k + (fb // 2 + 1))
                    cols = slice(fb * HALF, (fb + 1) * HALF)
                    wh, wl = (w[:, s, FF + fb * P:FF + (fb + 1) * P] for w in (w_hi, w_lo))
                    o = banks[4 + j % 2][:, :]
                    eng.matmul(o, wh, act_hi[:, j % 2, cols], start=(fb == 0), stop=False)
                    eng.matmul(o, wh, act_lo[:, j % 2, cols], start=False, stop=False)
                    mm = eng.matmul(o, wl, act_hi[:, j % 2, cols], start=False, stop=(fb == FB - 1))
                mm.then_inc(down_done, 1)

            up(0, 0)
            eng.wait_ge(gate_split, 1)
            for q in range(2):
                eng.wait_ge(t_split, q + 1)
                o, cols = banks[6 + q][0:NR, :], slice(q * HALF, (q + 1) * HALF)
                eng.matmul(o, gate_hi[:, :], t_hi[:, cols], start=True, stop=False)
                eng.matmul(o, gate_hi[:, :], t_lo[:, cols], start=False, stop=False)
                eng.matmul(o, gate_lo[:, :], t_hi[:, cols], start=False, stop=True).then_inc(gate_done, 1)

            def turn(i):
                for j in range(4):
                    if j < 3:
                        up(i, j + 1)
                    elif not isinstance(i, int) or i < NX // 2 - 1:
                        up(i + 1, 0)
                    if isinstance(i, int) and i == 0 and j == 0:
                        eng.wait_ge(logits_copied, 2)
                        for t in range(TILES):
                            mm = eng.transpose(banks[6][:, t * NR:(t + 1) * NR], logit_rows[:, t * P:(t + 1) * P],
                                               ident[0:NR, 0:NR])
                        mm.then_inc(logits_done, 1)
                    if isinstance(i, int) and i == 0 and j == 2:
                        eng.wait_ge(cw_ready, 1)
                        for t in range(TILES):
                            mm = eng.transpose(banks[6 + t // 4][0:NR, (t % 4) * P:(t % 4 + 1) * P], cw[:, t, :],
                                               ident[:, :])
                            if t % 4 == 3:
                                mm.then_inc(cwT_done, 1)
                    down(i, j)
            turns(eng, turn)
            eng.wait_ge(cw_copied, 2)
            for q in range(2):
                eng.wait_ge(acc_done, 2 * NX - 1 + q)
                transposes(banks[6 + q], lambda t: acc[:, t * P:(t + 1) * P], q, yT_done)


def kernel(x, L0_tok_weight, L0_tok_bias, L0_tok_mask, L0_ffn_gate_w, L0_ffn_gate_b, L0_ffn_sw1, L0_ffn_sb1,
           L0_ffn_sw2, L0_ffn_sb2, L0_ffn_rw1, L0_ffn_rb1, L0_ffn_rw2, L0_ffn_rb2):
    import numpy as np
    import concourse.bacc as bacc
    from concourse.bass_utils import run_bass_kernel_spmd

    c = np.ascontiguousarray
    weight = np.asarray(L0_tok_weight)
    order = [e for q in range(2) for el in range(2) for e in range(8 * el + 4 * q, 8 * el + 4 * q + 4)]
    rows = np.concatenate([np.asarray(L0_tok_mask), np.asarray(x).T,
                           weight[order].transpose(1, 0, 2).reshape(G, WCOLS)], axis=1)
    bias_row = np.concatenate([np.ones((1, W0), np.float32),
                               np.asarray(L0_tok_bias)[order].reshape(1, WCOLS)], axis=1)
    w1 = np.concatenate([np.asarray(L0_ffn_sw1), np.asarray(L0_ffn_rw1)])
    w2 = np.concatenate([np.asarray(L0_ffn_sw2), np.asarray(L0_ffn_rw2)])
    b1 = np.concatenate([np.asarray(L0_ffn_sb1), np.asarray(L0_ffn_rb1)])
    b2 = np.concatenate([np.asarray(L0_ffn_sb2), np.asarray(L0_ffn_rb2)])
    w2t = w2.transpose(0, 2, 1).reshape(NX, FB, P, P).transpose(0, 2, 1, 3).reshape(NX, P, FB * P)
    arrays = {
        "tiles": c(rows[:CHUNKS * P].reshape(CHUNKS, P, TCOLS)),
        "rest": c(np.concatenate([rows[CHUNKS * P:], bias_row])),
        "experts": c(np.concatenate([w1.transpose(0, 2, 1), w2t, b1.reshape(NX, FB, P).transpose(0, 2, 1),
                                     b2[:, :, None]], axis=2)),
        "gate_w": c(np.asarray(L0_ffn_gate_w).T),
        "gate_b": c(np.asarray(L0_ffn_gate_b).reshape(NR, 1)),
    }
    nc = bacc.Bacc("TRN2", target_bir_lowering=False, num_devices=1)
    args = [nc.dram_tensor(f"{n}_dram", a.shape, F32, kind="ExternalInput").ap() for n, a in arrays.items()]
    args.append(nc.dram_tensor("out_dram", (TOK, P), F32, kind="ExternalOutput").ap())
    build(nc, *args)
    r = run_bass_kernel_spmd(nc, [{f"{n}_dram": a for n, a in arrays.items()}], core_ids=[0])
    return r.results[0]["out_dram"].reshape(B, E, P)
```

```python
import concourse.bass as bass
from concourse import mybir
from contextlib import ExitStack

F32 = mybir.dt.float32
F32R = mybir.dt.float32r
ALU = mybir.AluOpType
ACT = mybir.ActivationFunctionType
AX = mybir.AxisListType

P = 128
B, E, G = 64, 16, 5000
CHUNKS = G // P
REST = G - CHUNKS * P + 1
WCOLS = E * P
W0 = P + B
TCOLS = W0 + WCOLS
RING = 6
LOOPS = CHUNKS // RING
TAIL = CHUNKS - LOOPS * RING
TAIL_LOADS = (((0, 4),), ((0, 2), (2, 4)), ((0, 1), (1, 2), (2, 3), (3, 4)))
TAIL_MASKS = ((0, 0, 0, 2), (0, 0, 2, 4), (1, 0, 0, 2), (1, 1, 2, 3), (2, 0, 0, 1), (2, 1, 1, 2), (2, 2, 2, 3),
              (2, 3, 3, 4))
POOL_MASK = (1, 1, 3, 4)
assert TAIL == len(TAIL_LOADS)
TOK = B * E
TILES = TOK // P
HALF = TOK // 2
NS, NR = 2, 8
NX = NS + NR
FF = 512
FB = FF // P
WX = FF + FB * P
XB = FB + 1
PIECES = ((0, 4), (4, 6), (6, 8))
WARM = (12, 3, 1, 2, 0, 6, 6, 2)
LN_EPS = 1e-05
NORM_EPS = 1e-12


def build(nc, tiles, rest, experts, gate_w, gate_b, out):
    ctx = ExitStack()
    with ctx:
        def sb(name, shape, dt=F32):
            return ctx.enter_context(nc.sbuf_tensor(name, shape, dt))

        def sem(name):
            return ctx.enter_context(nc.semaphore(name))

        ring = sb("ring", [P, RING, TCOLS])
        rest_tile = sb("rest_tile", [REST, TCOLS])
        ident = sb("ident", [P, P])
        block_mask = sb("block_mask", [P, P])
        ones = sb("ones", [P, P])
        gate_w_sb = sb("gate_w_sb", [P, NR])
        gate_hi = sb("gate_hi", [P, NR], F32R)
        gate_lo = sb("gate_lo", [P, NR], F32R)
        gate_b_sb = sb("gate_b_sb", [NR, 1])
        logit_rows = sb("logit_rows", [NR, TOK])
        zeros = sb("zeros", [P, XB])
        h_rows = sb("h_rows", [P, TILES, P])
        h_cols = sb("h_cols", [P, B, E])
        h_tok = sb("h_tok", [P, TILES, P])
        hn = sb("hn", [P, TILES, P + 1])
        xn = sb("xn", [P, TILES, P])
        xn_cols = sb("xn_cols", [P, TILES, P])
        sq = sb("sq", [P, TILES, P])
        ex = sb("ex", [P, TILES, P])
        attn = sb("attn", [P, TILES, P])
        h2 = sb("h2", [P, TILES, P])
        t_tok = h_rows
        t_hi = sb("t_hi", [P, TOK], F32R)
        t_lo = sb("t_lo", [P, TOK], F32R)
        stats = sb("stats", [P, 2, TILES, 6])
        mv = sb("mv", [P, 2, TILES, 2])
        eps = sb("eps", [P, 1])
        root = sb("root", [P, 4, TILES])
        small = sb("small", [P, 6, TILES])
        g_max = sb("g_max", [P, TILES])
        g_sh = sb("g_sh", [P, TILES, NR])
        g_ex = sb("g_ex", [P, TILES, NR])
        g_sum = sb("g_sum", [P, 2, TILES])
        before = sb("before", [P, TILES, NR, NR])
        rank = sb("rank", [P, 3, TILES, NR])
        cw = sb("cw", [P, TILES, NR])
        cw_cols = sb("cw_cols", [NR, TOK])
        one_rows = sb("one_rows", [NS, TOK])
        cw_dram = nc.dram_tensor("cw_dram", [NX, TOK], F32, kind="Internal").ap()
        w_raw = sb("w_raw", [P, 2, WX + XB])
        bias_now = sb("bias_now", [P, 2, XB])
        w_hi = sb("w_hi", [P, 2, WX], F32R)
        w_lo = sb("w_lo", [P, 2, WX], F32R)
        over = ring[:, :, :].rearrange("p r c -> p (r c)")
        act = over[:, 0:2 * FB * HALF].rearrange("p (s c) -> p s c", s=2)
        act_hi = sb("act_hi", [P, 2, FB * HALF], F32R)
        act_lo = sb("act_lo", [P, 2, FB * HALF], F32R)
        cwb = over[:, 2 * FB * HALF:2 * FB * HALF + 2 * TOK].rearrange("p (s c) -> p s c", s=2)
        part = sb("part", [P, 2, HALF])
        acc = sb("acc", [P, TOK])
        y = sb("y", [P, TILES, P])

        psum = ctx.enter_context(nc.psum_tensor("psum", [P, 8, 512], F32))
        banks = [psum[:, n, :] for n in range(8)]
        Y_BANKS = (6, 7, 4)
        LAST_BANKS = (5, 0)

        tile_loaded = [sem(f"tile_loaded{r}") for r in range(RING)]
        tail_loaded = [[sem(f"tail_loaded{r}_{n}") for n in range(len(TAIL_LOADS[r]))] for r in range(TAIL)]
        rest_loaded = sem("rest_loaded")
        rest_masked = sem("rest_masked")
        masked = sem("masked")
        pool_masked = sem("pool_masked")
        chunk_used = sem("chunk_used")
        h_summed = sem("h_summed")
        gate_loaded = sem("gate_loaded")
        const_step = sem("const_step")
        h_evacuated = [sem("h_evacuated0"), sem("h_evacuated1")]
        hT_done = sem("hT_done")
        hT_copied = [sem("hT_copied_act"), sem("hT_copied_dve")]
        htok_done = sem("htok_done")
        h_stats = sem("h_stats")
        h2_ready = sem("h2_ready")
        h2_stats = sem("h2_stats")
        htok_copied = sem("htok_copied")
        dve_link = sem("dve_link")
        var_ready = [sem("var_ready1"), sem("var_ready2")]
        root_ready = [sem("root_ready1"), sem("root_ready2")]
        scales_ready = [sem("scales_ready1"), sem("scales_ready2")]
        hn_scales = sem("hn_scales")
        hn_ready = sem("hn_ready")
        hn3_ready = sem("hn3_ready")
        xn_ready = [[sem("xn_ready0_12"), sem("xn_ready0_34")], [sem("xn_ready1_12"), sem("xn_ready1_34")]]
        xnT_done = sem("xnT_done")
        xnT_copied = sem("xnT_copied")
        gram_done = sem("gram_done")
        sq_done = sem("sq_done")
        ex_done = sem("ex_done")
        attn_ready = [sem("attn_ready0"), sem("attn_ready1")]
        ctx_done = sem("ctx_done")
        t_ready = [[sem("t_ready0_12"), sem("t_ready0_34")], [sem("t_ready1_12"), sem("t_ready1_34")]]
        tT_done = sem("tT_done")
        t_rounded = sem("t_rounded")
        t_split = sem("t_split")
        gate_rounded = sem("gate_rounded")
        gate_split = sem("gate_split")
        gate_done = sem("gate_done")
        logits_copied = sem("logits_copied")
        logits_done = sem("logits_done")
        g_shifted = sem("g_shifted")
        g_exped = sem("g_exped")
        cw_ready = sem("cw_ready")
        cwT_done = sem("cwT_done")
        cw_copied = sem("cw_copied")
        cw_stored = sem("cw_stored")
        w_loaded = [sem("w_loaded0"), sem("w_loaded1")]
        w_rounded = sem("w_rounded")
        w_split = sem("w_split")
        cwb_loaded = [sem("cwb_loaded0"), sem("cwb_loaded1")]
        up_done = sem("up_done")
        gelu_done = sem("gelu_done")
        act_rounded = [sem("act_rounded0"), sem("act_rounded1")]
        act_split = sem("act_split")
        down_done = sem("down_done")
        part_ready = sem("part_ready")
        acc_done = sem("acc_done")
        last_added = sem("last_added")
        yT_done = sem("yT_done")
        y_ready = sem("y_ready")
        out_stored = sem("out_stored")

        block = ctx.enter_context(nc.Block())

        def after(eng, s, value):
            if not isinstance(value, int) or value > 0:
                eng.wait_ge(s, value)

        def turns(eng, body):
            body(0)
            with eng.Fori(1, NX // 2 - 1) as i:
                body(i)
            body(NX // 2 - 1)

        tiled = lambda a: a.rearrange("p (t d) -> p t d", d=P)
        HT = (slice(0, TILES // 2), slice(TILES // 2, TILES))

        def reorder(copy, bank, h0, n, *func):
            src = bank[:, 0:n * P].rearrange("p (h l b) -> p l b h", h=n, l=2)
            dst = h_cols[:, :, :].rearrange("p b (l h) -> p l b h", l=2)[:, :, :, h0:h0 + n]
            return copy(dst, src, *func)

        def apply_mask(eng, tile, parts, e0, e1):
            w = tile[:, W0 + e0 * P:W0 + e1 * P].rearrange("p (e d) -> p e d", d=P)
            m = tile[:, 0:P].rearrange("p (o d) -> p o d", o=1).to_broadcast([parts, e1 - e0, P])
            return eng.tensor_tensor(w, w, m, ALU.mult)

        def attention_weights(eng, q):
            eng.wait_ge(const_step, 4)
            eng.wait_ge(ex_done, q + 1)
            m = block_mask[:, :].rearrange("p (o d) -> p o d", o=1).to_broadcast([P, 4, P])
            eng.tensor_tensor(attn[:, HT[q], :], ex[:, HT[q], :], m, ALU.mult).then_inc(attn_ready[q], 1)

        @block.sync
        def _(eng):
            for r in range(RING):
                eng.dma_start(ring[:, r, :], tiles[r]).then_inc(tile_loaded[r], 16)
                if r == 0:
                    eng.dma_start(rest_tile[:, :], rest).then_inc(rest_loaded, 16)
            with eng.Fori(1, LOOPS) as i:
                for r in range(RING):
                    eng.wait_ge(chunk_used, RING * i + (r + 1 - RING))
                    eng.dma_start(ring[:, r, :], tiles[bass.ds(RING * i + r, 1)].rearrange("a p c -> (a p) c"))\
                       .then_inc(tile_loaded[r], 16)
            for r in range(TAIL):
                eng.wait_ge(chunk_used, RING * (LOOPS - 1) + r + 1)
                for n, (c0, c1) in enumerate(TAIL_LOADS[r]):
                    cols = slice(W0 + 512 * c0 if n else 0, W0 + 512 * c1)
                    eng.dma_start(ring[:, r, cols], tiles[RING * LOOPS + r, :, cols]).then_inc(tail_loaded[r][n], 16)
            for x in range(2):
                eng.dma_start(w_raw[:, x, :], experts[x]).then_inc(w_loaded[x], 16)
            eng.wait_ge(const_step, 1)
            eng.dma_start(cw_dram[0:NS, :], one_rows[:, :]).then_inc(cw_stored, 16)
            eng.wait_ge(cw_stored, 16)
            eng.wait_ge(h_summed, 2)

            def turn(i):
                for s in range(2):
                    x = 2 * i + s
                    after(eng, part_ready, 2 * x - 2)
                    eng.dma_start(cwb[:, s, :], cw_dram[bass.ds(x, 1), :].to_broadcast([P, TOK]))\
                       .then_inc(cwb_loaded[s], 16)
                    if not isinstance(i, int) or i < NX // 2 - 1:
                        eng.wait_ge(w_split, 2 * x + 2)
                        eng.dma_start(w_raw[:, s, :], experts[bass.ds(x + 2, 1)].rearrange("a p c -> (a p) c"))\
                           .then_inc(w_loaded[s], 16)
                if isinstance(i, int) and i == 0:
                    eng.wait_ge(cw_copied, 2)
                    eng.dma_start(cw_dram[NS:NX, :], cw_cols[:, :]).then_inc(cw_stored, 16)
                    eng.wait_ge(cw_stored, 32)
            turns(eng, turn)
            for n, (t0, t1) in enumerate(PIECES):
                eng.wait_ge(y_ready, n + 1)
                eng.dma_start(out.rearrange("(t p) d -> p t d", p=P)[:, t0:t1, :], y[:, t0:t1, :])\
                   .then_inc(out_stored, 16)
            eng.wait_ge(out_stored, 16 * len(PIECES))

        @block.gpsimd
        def _(eng):
            eng.memset(one_rows[:, :], 1.0).then_inc(const_step, 1)
            eng.memset(ident[:, :], 0.0)
            eng.memset(block_mask[:, :], 1.0)
            eng.memset(ones[:, :], 1.0)
            eng.memset(hn[:, :, P:P + 1], 1.0)
            eng.memset(zeros[:, :], 0.0)
            eng.memset(eps[:, :], LN_EPS)
            eng.memset(acc[:, :], 0.0).then_inc(const_step, 1)
            eng.wait_ge(const_step, 2)
            eng.affine_select(out=ident[:, :], in_=ident[:, :], compare_op=ALU.not_equal, fill=1.0,
                              base=0, pattern=[[-1, P]], channel_multiplier=1)
            bm = block_mask[:, :].rearrange("p (n e) -> p n e", e=E)
            eng.affine_select(out=bm, in_=bm, compare_op=ALU.is_ge, fill=0.0, base=0,
                              pattern=[[-E, P // E], [0, E]], channel_multiplier=1).then_inc(const_step, 1)
            eng.wait_ge(const_step, 3)
            eng.affine_select(out=bm, in_=bm, compare_op=ALU.is_ge, fill=0.0, base=E - 1,
                              pattern=[[E, P // E], [0, E]], channel_multiplier=-1).then_inc(const_step, 1)

            r, n, c0, c1 = POOL_MASK
            eng.wait_ge(tail_loaded[r][0], 16)
            eng.wait_ge(tail_loaded[r][n], 16)
            apply_mask(eng, ring[:, r, :], P, 4 * c0, 4 * c1).then_inc(pool_masked, 1)

            def low_parts(part, s, x):
                eng.wait_ge(w_rounded, 2 * x + (part + 1))
                b, cols = (slice(0, FB), slice(FB, XB))[part], slice(part * FF, (part + 1) * FF)
                eng.tensor_tensor(bias_now[:, s, b], w_raw[:, s, WX + b.start:WX + b.stop], zeros[:, b], ALU.add)
                eng.tensor_tensor(w_lo[:, s, cols], w_raw[:, s, cols], w_hi[:, s, cols].bitcast(F32), ALU.subtract)\
                   .then_inc(w_split, 1)

            eng.wait_ge(gate_rounded, 1)
            eng.tensor_tensor(gate_lo[:, :], gate_w_sb[:, :], gate_hi[:, :].bitcast(F32), ALU.subtract)\
               .then_inc(gate_split, 1)
            eng.wait_ge(hn_scales, 1)
            eng.tensor_scalar(hn[:, 3, 0:P], h_tok[:, 3, :], mv[:, 0, 3, 0:1], small[:, 1, 3:4],
                              ALU.subtract, ALU.mult).then_inc(hn3_ready, 1)
            attention_weights(eng, 1)
            for x in range(2):
                for m in range(2):
                    low_parts(m, x, x)

            def turn(i):
                more = not isinstance(i, int) or i < NX // 2 - 1
                for j in range(4 if more else 3):
                    k = 4 * i + j
                    if j % 2 == 0 and more:
                        eng.wait_ge(gelu_done, FB * (k + 2))
                        low_parts(0, j // 2, 2 * i + (j // 2 + 2))
                    eng.wait_ge(part_ready, k + 1)
                    after(eng, acc_done, k - 1)
                    half = acc[:, (j % 2) * HALF:(j % 2 + 1) * HALF]
                    eng.tensor_tensor(half, half, part[:, j % 2, :], ALU.add).then_inc(acc_done, 1)
                    if j % 2 and more:
                        low_parts(1, j // 2, 2 * i + (j // 2 + 2))
            turns(eng, turn)

        @block.scalar
        def _(eng):
            eng.dma_start(gate_w_sb[:, :], gate_w).then_inc(gate_loaded, 16)
            eng.dma_start(gate_b_sb[:, :], gate_b).then_inc(gate_loaded, 16)
            eng.wait_ge(const_step, 2)
            eng.activation(root[:, 3, 0:1], ones[:, 0:1], ACT.Sqrt)
            eng.wait_ge(gate_loaded, 32)
            eng.activation(gate_hi[:, :], gate_w_sb[:, :], ACT.Copy).then_inc(gate_rounded, 1)
            eng.wait_ge(h_summed, 2)
            eng.activation(h_rows[:, 4:8, :], tiled(banks[1][:, :]), ACT.Copy).then_inc(h_evacuated[1], 1)
            eng.wait_ge(hT_done, 1)
            reorder(eng.activation, banks[2], 0, 4, ACT.Copy).then_inc(hT_copied[0], 1)
            eng.wait_ge(hT_done, 2)
            reorder(eng.activation, banks[7], 6, 2, ACT.Copy).then_inc(hT_copied[0], 1)

            def h_tok_copy(q):
                eng.wait_ge(h_stats, 4 * q + 4)
                eng.activation(h_tok[:, 4 * q:4 * q + 4, :], tiled(banks[4 + q][:, :]), ACT.Copy)\
                   .then_inc(htok_copied, 1)

            def root1(q):
                eng.wait_ge(var_ready[0], q + 1)
                eng.activation(root[:, 1, HT[q]], mv[:, 0, HT[q], 1], ACT.Sqrt, scale=float(P))
                eng.activation(root[:, 0, HT[q]], mv[:, 0, HT[q], 1], ACT.Sqrt, bias=eps[:, :])\
                   .then_inc(root_ready[0], 1)

            def scores(q):
                eng.wait_ge(gram_done, q + 1)
                eng.activation(sq[:, HT[q], :], tiled(banks[q][:, :]), ACT.Square).then_inc(sq_done, 1)
                eng.wait_ge(sq_done, q + 1)
                eng.activation(ex[:, HT[q], :], sq[:, HT[q], :], ACT.Exp).then_inc(ex_done, 1)

            h_tok_copy(0)
            root1(0)
            h_tok_copy(1)
            eng.wait_ge(scales_ready[0], 1)
            for t in (2, 3):
                n = eng.activation(xn[:, t, :], h_tok[:, t, :], ACT.Identity, scale=small[:, 2, t:t + 1],
                                   bias=small[:, 3, t:t + 1])
            n.then_inc(xn_ready[0][1], 1)
            root1(1)
            eng.activation(root[:, 3, 2:3], ones[:, 0:1], ACT.Exp)
            eng.wait_ge(scales_ready[0], 2)
            for t in (6, 7):
                n = eng.activation(xn[:, t, :], h_tok[:, t, :], ACT.Identity, scale=small[:, 2, t:t + 1],
                                   bias=small[:, 3, t:t + 1])
            n.then_inc(xn_ready[1][1], 1)
            scores(0)
            scores(1)

            def high_parts(part, s, x):
                cols = slice(part * FF, (part + 1) * FF)
                if part == 0:
                    eng.wait_ge(w_loaded[s], 8 * (x - s) + 16 if isinstance(x, int) else 8 * x + (16 - 8 * s))
                    after(eng, gelu_done, 2 * FB * (x - 1))
                else:
                    after(eng, down_done, 2 * (x - 1))
                eng.activation(w_hi[:, s, cols], w_raw[:, s, cols], ACT.Copy).then_inc(w_rounded, 1)

            def root2(q):
                eng.wait_ge(var_ready[1], q + 1)
                eng.activation(root[:, 2, HT[q]], mv[:, 1, HT[q], 1], ACT.Sqrt, bias=eps[:, :])\
                   .then_inc(root_ready[1], 1)

            def t_high(q):
                eng.wait_ge(tT_done, q + 1)
                eng.activation(t_hi[:, q * HALF:(q + 1) * HALF], banks[6 + q][:, :], ACT.Copy).then_inc(t_rounded, 1)

            eng.activation(root[:, 3, 1:2], ones[:, 0:1], ACT.Sqrt)
            for m in range(2):
                high_parts(m, 0, 0)
            root2(0)
            eng.wait_ge(scales_ready[1], 1)
            for t in (2, 3):
                n = eng.activation(t_tok[:, t, :], h2[:, t, :], ACT.Identity, scale=small[:, 4, t:t + 1],
                                   bias=small[:, 5, t:t + 1])
            n.then_inc(t_ready[0][1], 1)
            t_high(0)
            root2(1)
            eng.activation(root[:, 3, 3:4], ones[:, 0:1], ACT.Gelu)

            def gelu(i, j):
                k = 4 * i + j
                after(eng, act_split, 2 * k - 2)
                for fb in range(FB):
                    if fb == 1 and isinstance(k, int) and k == 0:
                        t_high(1)
                    eng.wait_ge(up_done, FB * k + (fb + 1))
                    eng.activation(act[:, j % 2, fb * HALF:(fb + 1) * HALF], banks[fb][:, :], ACT.Gelu,
                                   bias=bias_now[:, j // 2, fb:fb + 1]).then_inc(gelu_done, 1)
                after(eng, down_done, k - 1)
                eng.wait_ge(gelu_done, FB * k + FB)
                eng.activation(act_hi[:, j % 2, 2 * HALF:], act[:, j % 2, 2 * HALF:], ACT.Copy)\
                   .then_inc(act_rounded[1], 1)

            def turn(i):
                first = isinstance(i, int) and i == 0
                last = isinstance(i, int) and i == NX // 2 - 1
                for j in range(4):
                    gelu(i, j)
                    if first and j == 0:
                        high_parts(0, 1, 1)
                        high_parts(1, 1, 1)
                    if first and j == 1:
                        for q in range(2):
                            eng.wait_ge(gate_done, q + 1)
                            eng.activation(logit_rows[:, q * HALF:(q + 1) * HALF], banks[6 + q][0:NR, :],
                                           ACT.Identity, bias=gate_b_sb[:, :]).then_inc(logits_copied, 1)
                    if first and j == 2:
                        eng.wait_ge(g_shifted, 1)
                        eng.activation(g_ex[:, :, :], g_sh[:, :, :], ACT.Exp).then_inc(g_exped, 1)
                    if j % 2 and not last:
                        high_parts(0, j // 2, 2 * i + (j // 2 + 2))
                    if j == 2 and not last:
                        high_parts(1, 0, 2 * i + 2)
                    if j == 0 and not first:
                        high_parts(1, 1, 2 * i + 1)
                    if first and j == 3:
                        for q in range(2):
                            eng.wait_ge(cwT_done, q + 1)
                            eng.activation(cw_cols[:, q * HALF:(q + 1) * HALF], banks[6 + q][0:NR, :], ACT.Copy)\
                               .then_inc(cw_copied, 1)
            turns(eng, turn)

        @block.vector
        def _(eng):
            links = [0]

            def mark(ins):
                links[0] += 1
                ins.then_inc(dve_link, 1)
                return links[0]

            def link(ins):
                eng.wait_ge(dve_link, mark(ins))

            eng.wait_ge(rest_loaded, 16)
            apply_mask(eng, rest_tile, REST, 0, E).then_inc(rest_masked, 1)
            with eng.Fori(0, LOOPS) as i:
                for r in range(RING):
                    eng.wait_ge(tile_loaded[r], 16 * i + 16)
                    apply_mask(eng, ring[:, r, :], P, 0, E).then_inc(masked, 1)
            for r, n, c0, c1 in TAIL_MASKS:
                eng.wait_ge(tail_loaded[r][n], 16)
                apply_mask(eng, ring[:, r, :], P, 4 * c0, 4 * c1).then_inc(masked, 1)

            eng.wait_ge(h_summed, 1)
            eng.tensor_copy(h_rows[:, 0:4, :], tiled(banks[0][:, :])).then_inc(h_evacuated[0], 1)
            eng.wait_ge(hT_done, 2)
            reorder(eng.tensor_copy, banks[3], 4, 2).then_inc(hT_copied[1], 1)

            def norm_aggregate(n, q):
                for t in range(4 * q, 4 * q + 4):
                    eng.wait_ge((h_stats, h2_stats)[n], t + 1)
                    a = eng.bn_aggr(mv[:, n, t, :], stats[:, n, t, :])
                a.then_inc(var_ready[n], 1)

            def statistics1(q):
                eng.wait_ge(htok_done, q + 1)
                for n in range(4):
                    eng.bn_stats(stats[:, 0, 4 * q + n, :], banks[4 + q][:, n * P:(n + 1) * P]).then_inc(h_stats, 1)

            def normed(n, dst, tiles_, row):
                src = (h_tok, h2)[n]
                for t in tiles_:
                    s = eng.tensor_scalar(dst[:, t, 0:P], src[:, t, :], mv[:, n, t, 0:1], small[:, row, t:t + 1],
                                          ALU.subtract, ALU.mult)
                return s

            def scales1(q):
                eng.wait_ge(root_ready[0], q + 1)
                link(eng.scalar_tensor_tensor(out=small[:, 0, HT[q]], in0=root[:, 0, HT[q]], scalar=NORM_EPS,
                                              in1=root[:, 1, HT[q]], op0=ALU.mult, op1=ALU.add))
                link(eng.reciprocal(small[:, 2, HT[q]], small[:, 0, HT[q]]))
                eng.scalar_tensor_tensor(out=small[:, 3, HT[q]], in0=mv[:, 0, HT[q], 0], scalar=-1.0,
                                         in1=small[:, 2, HT[q]], op0=ALU.mult, op1=ALU.mult)\
                   .then_inc(scales_ready[0], 1)
                eng.wait_ge(htok_copied, q + 1)
                normed(0, xn, (4 * q, 4 * q + 1), 2).then_inc(xn_ready[q][0], 1)

            def xn_turned(q):
                eng.wait_ge(xnT_done, q + 1)
                eng.tensor_copy(xn_cols[:, HT[q], :], tiled(banks[6 + q][:, :])).then_inc(xnT_copied, 1)

            statistics1(0)
            norm_aggregate(0, 0)
            statistics1(1)
            scales1(0)
            norm_aggregate(0, 1)
            xn_turned(0)
            scales1(1)
            eng.reciprocal(small[:, 1, :], root[:, 0, :]).then_inc(hn_scales, 1)
            eng.wait_ge(hn_scales, 1)
            normed(0, hn, (0, 1), 1)
            xn_turned(1)
            normed(0, hn, (2,), 1).then_inc(hn_ready, 1)
            attention_weights(eng, 0)
            normed(0, hn, (4, 5, 6, 7), 1).then_inc(hn_ready, 1)

            def denominators(q):
                eng.wait_ge(ctx_done, q + 1)
                link(eng.reciprocal(g_sum[:, 0, HT[q]].rearrange("p (a b) -> p a b", b=2),
                                    psum[:, 2 + 2 * q:4 + 2 * q, P:2 * P + 2:P + 1]))

            def residual(*tiles_):
                for t in tiles_:
                    c = (t % 2) * (P + 1)
                    eng.scalar_tensor_tensor(out=h2[:, t, :], in0=banks[2 + t // 2][:, c:c + P],
                                             scalar=g_sum[:, 0, t:t + 1], in1=h_tok[:, t, :],
                                             op0=ALU.mult, op1=ALU.add).then_inc(h2_ready, 1)

            def statistics2(q):
                for t in range(4 * q, 4 * q + 4):
                    eng.wait_ge(h2_ready, t + 1)
                    eng.bn_stats(stats[:, 1, t, :], h2[:, t, :]).then_inc(h2_stats, 1)

            def scales2(q):
                eng.wait_ge(root_ready[1], q + 1)
                link(eng.reciprocal(small[:, 4, HT[q]], root[:, 2, HT[q]]))
                s = eng.scalar_tensor_tensor(out=small[:, 5, HT[q]], in0=mv[:, 1, HT[q], 0], scalar=-1.0,
                                             in1=small[:, 4, HT[q]], op0=ALU.mult, op1=ALU.mult)
                s.then_inc(scales_ready[1], 1)

            def t_low(q):
                cols = slice(q * HALF, (q + 1) * HALF)
                eng.wait_ge(t_rounded, q + 1)
                eng.tensor_tensor(t_lo[:, cols], banks[6 + q][:, :], t_hi[:, cols].bitcast(F32), ALU.subtract)\
                   .then_inc(t_split, 1)

            denominators(0)
            residual(0, 1, 2, 3)
            statistics2(0)
            norm_aggregate(1, 0)
            scales2(0)
            normed(1, t_tok, (0, 1), 4).then_inc(t_ready[0][0], 1)
            denominators(1)
            residual(4, 5, 6, 7)
            statistics2(1)
            norm_aggregate(1, 1)
            t_low(0)
            scales2(1)
            normed(1, t_tok, (4, 5), 4).then_inc(t_ready[1][0], 1)
            normed(1, t_tok, (6, 7), 4).then_inc(t_ready[1][1], 1)
            t_low(1)

            per_tile = lambda a: a.rearrange("p (t o) -> p t o", o=1).to_broadcast([P, TILES, NR])

            def router_shift():
                eng.wait_ge(logits_done, 1)
                logits = banks[6][:, 0:TILES * NR].rearrange("p (t e) -> p t e", e=NR)
                link(eng.tensor_reduce(g_max[:, :], logits, AX.X, ALU.max))
                eng.tensor_tensor(g_sh[:, :, :], logits, per_tile(g_max[:, :]), ALU.subtract).then_inc(g_shifted, 1)

            def router():
                eng.wait_ge(g_exped, 1)
                for e in range(NR):
                    for f0, f1, op in ((0, e, ALU.is_ge), (e, NR, ALU.is_gt)):
                        if f1 > f0:
                            c = eng.tensor_tensor(before[:, :, e, f0:f1], g_ex[:, :, f0:f1],
                                                  g_ex[:, :, e:e + 1].to_broadcast([P, TILES, f1 - f0]), op)
                compared = mark(c)
                eng.tensor_reduce(g_sum[:, 0, :], g_ex[:, :, :], AX.X, ALU.add)
                eng.wait_ge(dve_link, compared)
                link(eng.tensor_reduce(rank[:, 0, :, :], before[:, :, :, :], AX.X, ALU.add))
                eng.reciprocal(g_sum[:, 1, :], g_sum[:, 0, :])
                link(eng.tensor_scalar(rank[:, 1, :, :], rank[:, 0, :, :], 2.0, None, ALU.is_lt))
                link(eng.tensor_tensor(rank[:, 2, :, :], rank[:, 1, :, :], g_ex[:, :, :], ALU.mult))
                eng.tensor_tensor(cw[:, :, :], rank[:, 2, :, :], per_tile(g_sum[:, 1, :]), ALU.mult)\
                   .then_inc(cw_ready, 1)

            def split_act(i, j):
                k = 4 * i + j
                eng.wait_ge(gelu_done, FB * k + 2)
                after(eng, down_done, k - 1)
                first, second = slice(0, 2 * HALF), slice(2 * HALF, 4 * HALF)
                eng.tensor_copy(act_hi[:, j % 2, first], act[:, j % 2, first]).then_inc(act_rounded[0], 1)
                for rounded, cols in zip(act_rounded, (first, second)):
                    eng.wait_ge(rounded, k + 1)
                    eng.tensor_tensor(act_lo[:, j % 2, cols], act[:, j % 2, cols],
                                      act_hi[:, j % 2, cols].bitcast(F32), ALU.subtract).then_inc(act_split, 1)

            def weigh(i, j):
                k = 4 * i + j
                s = j // 2
                eng.wait_ge(down_done, k + 1)
                eng.wait_ge(cwb_loaded[s], 16 * i + 16)
                after(eng, acc_done, k - 1)
                eng.scalar_tensor_tensor(out=part[:, j % 2, :], in0=banks[4 + j % 2][:, :],
                                         scalar=bias_now[:, s, FB:XB],
                                         in1=cwb[:, s, (j % 2) * HALF:(j % 2 + 1) * HALF],
                                         op0=ALU.add, op1=ALU.mult).then_inc(part_ready, 1)

            split_act(0, 0)

            def turn(i):
                for j in range(4):
                    if isinstance(i, int) and i == 0 and j == 1:
                        router_shift()
                    if isinstance(i, int) and i == 0 and j == 2:
                        router()
                    if j < 3:
                        split_act(i, j + 1)
                    elif not isinstance(i, int) or i < NX // 2 - 1:
                        split_act(i + 1, 0)
                    if j < 3 or not isinstance(i, int) or i < NX // 2 - 1:
                        weigh(i, j)
            turns(eng, turn)

            def finish(n):
                t0, t1 = PIECES[n]
                eng.wait_ge(yT_done, n + 1)
                eng.tensor_tensor(y[:, t0:t1, :], tiled(banks[Y_BANKS[n]][:, 0:(t1 - t0) * P]), h2[:, t0:t1, :], ALU.add)\
                   .then_inc(y_ready, 1)

            last = 2 * NX - 1
            eng.wait_ge(acc_done, last - 1)
            for n in range(2):
                cols = slice(HALF + n * HALF // 2, HALF + (n + 1) * HALF // 2)
                own = slice(cols.start - HALF, cols.stop - HALF)
                eng.wait_ge(down_done, last + n + 1)
                weighted = mark(eng.scalar_tensor_tensor(out=part[:, 1, own],
                                                         in0=banks[LAST_BANKS[n]][:, 0:HALF // 2],
                                                         scalar=bias_now[:, 1, FB:XB], in1=cwb[:, 1, cols],
                                                         op0=ALU.add, op1=ALU.mult))
                if n:
                    finish(0)
                eng.wait_ge(dve_link, weighted)
                eng.tensor_tensor(acc[:, cols], acc[:, cols], part[:, 1, own], ALU.add).then_inc(last_added, 1)
            finish(1)
            finish(2)

        @block.tensor
        def _(eng):
            def quarter(tile, parts, n, start, stop):
                c, el = W0 + n * 512, n % 2
                return eng.matmul(banks[n // 2][el * B:(el + 1) * B, :], tile[0:parts, P:W0],
                                  tile[0:parts, c:c + 512], start=start, stop=stop)

            def chunk(tile, parts, q, start, stop):
                quarter(tile, parts, 2 * q, start, stop)
                return quarter(tile, parts, 2 * q + 1, start, stop)

            eng.wait_ge(rest_masked, 1)
            for q in range(2):
                chunk(rest_tile, REST, q, True, False)
            with eng.Fori(0, LOOPS) as i:
                for r in range(RING):
                    eng.wait_ge(masked, RING * i + (r + 1))
                    for q in range(2):
                        mm = chunk(ring[:, r, :], P, q, False, False)
                    mm.then_inc(chunk_used, 1)
            for n, (r, _, c0, c1) in enumerate(TAIL_MASKS):
                eng.wait_ge(masked, RING * LOOPS + n + 1)
                for c in range(c0, c1):
                    mm = quarter(ring[:, r, :], P, c, False, r == TAIL - 1)
                    if r == TAIL - 1 and c % 2:
                        mm.then_inc(h_summed, 1)
                if (r, c1) == (POOL_MASK[0], POOL_MASK[2]):
                    eng.wait_ge(pool_masked, 1)
                    quarter(ring[:, r, :], P, POOL_MASK[2], False, False)

            def transposes(dst, src, q, done, second=None):
                for n in range(4):
                    if n == 2 and second is not None:
                        eng.wait_ge(second, 1)
                    mm = eng.transpose(dst[:, n * P:(n + 1) * P], src(4 * q + n), ident[:, :])
                mm.then_inc(done, 1)

            def keep_warm(n, bank):
                for _ in range(n):
                    eng.matmul(banks[bank][:, 0:P], ident[:, :], ident[:, :], start=True, stop=True)

            eng.wait_ge(const_step, 4)
            eng.wait_ge(h_evacuated[0], 1)
            transposes(banks[2], lambda t: h_rows[:, t, :], 0, hT_done)
            eng.wait_ge(h_evacuated[1], 1)
            for n in range(4):
                mm = eng.transpose(banks[3 if n < 2 else 7][:, (n % 2) * P:(n % 2 + 1) * P], h_rows[:, 4 + n, :],
                                   ident[:, :])
            mm.then_inc(hT_done, 1)
            eng.wait_ge(hT_copied[0], 2)
            eng.wait_ge(hT_copied[1], 1)
            for q in range(2):
                transposes(banks[4 + q], lambda t: h_cols[:, 8 * t:8 * t + 8, :], q, htok_done)
            keep_warm(WARM[0], 2)
            for q in range(2):
                eng.wait_ge(xn_ready[q][0], 1)
                transposes(banks[6 + q], lambda t: xn[:, t, :], q, xnT_done, xn_ready[q][1])
                keep_warm(WARM[1 + 2 * q], 2)
                eng.wait_ge(xnT_copied, q + 1)
                for n in range(4):
                    t = 4 * q + n
                    mm = eng.matmul(banks[q][:, n * P:(n + 1) * P], xn_cols[:, t, :], xn_cols[:, t, :],
                                    start=True, stop=True)
                mm.then_inc(gram_done, 1)
                keep_warm(WARM[2 + 2 * q], 2)
            for q in range(2):
                eng.wait_ge(hn_ready, q + 1)
                if q == 0:
                    eng.wait_ge(hn3_ready, 1)
                eng.wait_ge(attn_ready[q], 1)
                for n in range(4):
                    t = 4 * q + n
                    c = (t % 2) * (P + 1)
                    mm = eng.matmul(banks[2 + t // 2][:, c:c + P + 1], attn[:, t, :], hn[:, t, :],
                                    start=True, stop=True)
                mm.then_inc(ctx_done, 1)
                keep_warm(WARM[5 + q], 0)

            def t_transposed(q):
                eng.wait_ge(t_ready[q][0], 1)
                transposes(banks[6 + q], lambda t: t_tok[:, t, :], q, tT_done, t_ready[q][1])

            def up(i, j):
                k = 4 * i + j
                s, cols = (j // 2) % 2, slice((j % 2) * HALF, (j % 2 + 1) * HALF)
                if j % 2 == 0:
                    eng.wait_ge(w_split, 4 * i + (j + 1))
                if isinstance(k, int) and k < 2:
                    eng.wait_ge(t_rounded, k + 1)
                first = isinstance(k, int) and k == 0
                for fb in range(FB):
                    after(eng, gelu_done, FB * k + (fb + 1 - FB))
                    wh, wl = (w[:, s, fb * P:(fb + 1) * P] for w in (w_hi, w_lo))
                    eng.matmul(banks[fb][:, :], wh, t_hi[:, cols], start=True, stop=False)
                    eng.matmul(banks[fb][:, :], wl, t_hi[:, cols], start=False, stop=False)
                    if not first:
                        if fb == 0 and isinstance(k, int) and k == 1:
                            eng.wait_ge(t_split, 2)
                        eng.matmul(banks[fb][:, :], wh, t_lo[:, cols], start=False, stop=True).then_inc(up_done, 1)
                if first:
                    eng.wait_ge(t_split, 1)
                    for fb in range(FB):
                        if fb == FB // 2:
                            t_transposed(1)
                        eng.matmul(banks[fb][:, :], w_hi[:, s, fb * P:(fb + 1) * P], t_lo[:, cols],
                                   start=False, stop=True).then_inc(up_done, 1)

            def down(i, j):
                k = 4 * i + j
                s = j // 2
                if j % 2 == 0:
                    eng.wait_ge(w_split, 4 * i + (j + 2))
                after(eng, part_ready, k - 1)
                for fb in range(FB):
                    if fb % 2 == 0:
                        eng.wait_ge(act_split, 2 * k + (fb // 2 + 1))
                    cols = slice(fb * HALF, (fb + 1) * HALF)
                    wh, wl = (w[:, s, FF + fb * P:FF + (fb + 1) * P] for w in (w_hi, w_lo))
                    o = banks[4 + j % 2][:, :]
                    eng.matmul(o, wh, act_hi[:, j % 2, cols], start=(fb == 0), stop=False)
                    eng.matmul(o, wh, act_lo[:, j % 2, cols], start=False, stop=False)
                    mm = eng.matmul(o, wl, act_hi[:, j % 2, cols], start=False, stop=(fb == FB - 1))
                mm.then_inc(down_done, 1)

            def router_logits(q):
                eng.wait_ge(gate_split, 1)
                eng.wait_ge(t_split, q + 1)
                o, cols = banks[6 + q][0:NR, :], slice(q * HALF, (q + 1) * HALF)
                eng.matmul(o, gate_hi[:, :], t_hi[:, cols], start=True, stop=False)
                eng.matmul(o, gate_hi[:, :], t_lo[:, cols], start=False, stop=False)
                eng.matmul(o, gate_lo[:, :], t_hi[:, cols], start=False, stop=True).then_inc(gate_done, 1)

            t_transposed(0)
            keep_warm(WARM[7], 0)
            up(0, 0)
            router_logits(0)

            def back(n):
                for c, t in enumerate(range(*PIECES[n])):
                    mm = eng.transpose(banks[Y_BANKS[n]][:, c * P:(c + 1) * P], acc[:, t * P:(t + 1) * P], ident[:, :])
                mm.then_inc(yT_done, 1)

            def turn(i):
                for j in range(4):
                    if j < 3:
                        up(i, j + 1)
                    elif not isinstance(i, int) or i < NX // 2 - 1:
                        up(i + 1, 0)
                    if isinstance(i, int) and i == 0 and j == 0:
                        router_logits(1)
                    if isinstance(i, int) and i == 0 and j == 1:
                        eng.wait_ge(logits_copied, 2)
                        for t in range(TILES):
                            mm = eng.transpose(banks[6][:, t * NR:(t + 1) * NR], logit_rows[:, t * P:(t + 1) * P],
                                               ident[0:NR, 0:NR])
                        mm.then_inc(logits_done, 1)
                    if isinstance(i, int) and i == 0 and j == 3:
                        eng.wait_ge(cw_ready, 1)
                        for t in range(TILES):
                            mm = eng.transpose(banks[6 + t // 4][0:NR, (t % 4) * P:(t % 4 + 1) * P], cw[:, t, :],
                                               ident[:, :])
                            if t % 4 == 3:
                                mm.then_inc(cwT_done, 1)
                    if j < 3 or not isinstance(i, int) or i < NX // 2 - 1:
                        down(i, j)
            turns(eng, turn)
            eng.wait_ge(part_ready, 2 * NX - 2)
            for fb0 in (0, FB // 2):
                eng.wait_ge(act_split, 2 * (2 * NX - 1) + (1 if fb0 == 0 else 2))
                for n in range(2):
                    for fb in range(fb0, fb0 + FB // 2):
                        cols = slice(fb * HALF + n * HALF // 2, fb * HALF + (n + 1) * HALF // 2)
                        wh, wl = (w[:, 1, FF + fb * P:FF + (fb + 1) * P] for w in (w_hi, w_lo))
                        o = banks[LAST_BANKS[n]][:, 0:HALF // 2]
                        eng.matmul(o, wh, act_hi[:, 1, cols], start=(fb == 0), stop=False)
                        eng.matmul(o, wl, act_hi[:, 1, cols], start=False, stop=False)
                        mm = eng.matmul(o, wh, act_lo[:, 1, cols], start=False, stop=(fb == FB - 1))
                    if fb0:
                        mm.then_inc(down_done, 1)
            eng.wait_ge(acc_done, 2 * NX - 1)
            back(0)
            for n in (1, 2):
                eng.wait_ge(last_added, n)
                back(n)


def kernel(x, L0_tok_weight, L0_tok_bias, L0_tok_mask, L0_ffn_gate_w, L0_ffn_gate_b, L0_ffn_sw1, L0_ffn_sb1,
           L0_ffn_sw2, L0_ffn_sb2, L0_ffn_rw1, L0_ffn_rb1, L0_ffn_rw2, L0_ffn_rb2):
    import numpy as np
    import concourse.bacc as bacc
    from concourse.bass_utils import run_bass_kernel_spmd

    c = np.ascontiguousarray
    weight = np.asarray(L0_tok_weight)
    order = [e for q in range(2) for el in range(2) for e in range(8 * el + 4 * q, 8 * el + 4 * q + 4)]
    rows = np.concatenate([np.asarray(L0_tok_mask), np.asarray(x).T,
                           weight[order].transpose(1, 0, 2).reshape(G, WCOLS)], axis=1)
    bias_row = np.concatenate([np.ones((1, W0), np.float32),
                               np.asarray(L0_tok_bias)[order].reshape(1, WCOLS)], axis=1)
    w1 = np.concatenate([np.asarray(L0_ffn_sw1), np.asarray(L0_ffn_rw1)])
    w2 = np.concatenate([np.asarray(L0_ffn_sw2), np.asarray(L0_ffn_rw2)])
    b1 = np.concatenate([np.asarray(L0_ffn_sb1), np.asarray(L0_ffn_rb1)])
    b2 = np.concatenate([np.asarray(L0_ffn_sb2), np.asarray(L0_ffn_rb2)])
    w2t = w2.transpose(0, 2, 1).reshape(NX, FB, P, P).transpose(0, 2, 1, 3).reshape(NX, P, FB * P)
    arrays = {
        "tiles": c(rows[:CHUNKS * P].reshape(CHUNKS, P, TCOLS)),
        "rest": c(np.concatenate([rows[CHUNKS * P:], bias_row])),
        "experts": c(np.concatenate([w1.transpose(0, 2, 1), w2t, b1.reshape(NX, FB, P).transpose(0, 2, 1),
                                     b2[:, :, None]], axis=2)),
        "gate_w": c(np.asarray(L0_ffn_gate_w).T),
        "gate_b": c(np.asarray(L0_ffn_gate_b).reshape(NR, 1)),
    }
    nc = bacc.Bacc("TRN2", target_bir_lowering=False, num_devices=1)
    args = [nc.dram_tensor(f"{n}_dram", a.shape, F32, kind="ExternalInput").ap() for n, a in arrays.items()]
    args.append(nc.dram_tensor("out_dram", (TOK, P), F32, kind="ExternalOutput").ap())
    build(nc, *args)
    r = run_bass_kernel_spmd(nc, [{f"{n}_dram": a for n, a in arrays.items()}], core_ids=[0])
    return r.results[0]["out_dram"].reshape(B, E, P)
```
